# Optimizing a Trainium2 kernel written in Bass

```python
import numpy as np
import jax
import jax.numpy as jnp

def _softmax(x, axis=-1):
    return jax.nn.softmax(x, axis=axis)

def _gelu(x):
    return jax.nn.gelu(x, approximate=True)

def _silu(x):
    return jax.nn.silu(x)

def _sigmoid(x):
    return jax.nn.sigmoid(x)

def _layernorm(x, axis=-1, eps=1e-05):
    m = jnp.mean(x, axis=axis, keepdims=True)
    v = jnp.var(x, axis=axis, keepdims=True)
    return (x - m) / jnp.sqrt(v + eps)

def _scatter_add(tgt, idx, src, axis=0):
    return tgt.at[idx].add(src)

def _segment_sum(src, seg, n):
    return jax.ops.segment_sum(src, seg, n)
kernel_name = 'mk_seq_postln_d1_jaxref_r4_5f08f1'

def setup_inputs(seed: int=0):
    np.random.seed(seed)
    _w = jnp.asarray

    def _L0_attn_setup():
        import jax, jax.numpy as jnp
        import numpy as np
        from jax import lax
        B, L, D = (4, 512, 256)
        DSTATE, DCONV, EXPAND, NGROUPS, CHUNK = (128, 4, 2, 1, 64)
        HEADDIM = 64
        DINNER = EXPAND * D
        NHEADS = DINNER // HEADDIM
        CONVDIM = DINNER + 2 * NGROUPS * DSTATE
        DINPROJ = 2 * DINNER + 2 * NGROUPS * DSTATE + NHEADS
        EPS_OUT = 1.1920929e-07
        EPS_GATE = 1e-05

        def rmsnorm(x, eps):
            return x * lax.rsqrt(jnp.mean(x * x, -1, keepdims=True) + eps)

        def segsum(x):
            c = x.shape[-1]
            xc = jnp.cumsum(x, -1)
            d = xc[..., :, None] - xc[..., None, :]
            mask = jnp.tril(jnp.ones((c, c), bool))
            return jnp.where(mask, d, -jnp.inf)

        def mamba2(xn, w_in, conv_w, conv_b, dt_bias, a_log, d_skip, norm_w, w_out):
            b, l, _ = xn.shape
            zxbcdt = xn @ w_in
            z = zxbcdt[..., :DINNER]
            xbc = zxbcdt[..., DINNER:DINNER + CONVDIM]
            dt_raw = zxbcdt[..., DINNER + CONVDIM:]
            xp = jnp.pad(xbc, ((0, 0), (DCONV - 1, 0), (0, 0)))
            xc = sum((xp[:, k:k + l, :] * conv_w[:, k] for k in range(DCONV))) + conv_b
            xc = jax.nn.silu(xc)
            xh = xc[..., :DINNER].reshape(b, l, NHEADS, HEADDIM)
            Bm = xc[..., DINNER:DINNER + NGROUPS * DSTATE].reshape(b, l, NGROUPS, DSTATE)
            Cm = xc[..., DINNER + NGROUPS * DSTATE:].reshape(b, l, NGROUPS, DSTATE)
            hpg = NHEADS // NGROUPS
            Bh = jnp.repeat(Bm, hpg, 2)
            Ch = jnp.repeat(Cm, hpg, 2)
            dt = jax.nn.softplus(dt_raw + dt_bias)
            a = dt * -jnp.exp(a_log)
            u = dt[..., None] * xh
            nc = l // CHUNK
            uc = u.reshape(b, nc, CHUNK, NHEADS, HEADDIM)
            Bc = Bh.reshape(b, nc, CHUNK, NHEADS, DSTATE)
            Cc = Ch.reshape(b, nc, CHUNK, NHEADS, DSTATE)
            ac = a.reshape(b, nc, CHUNK, NHEADS).transpose(0, 3, 1, 2)
            a_cum = jnp.cumsum(ac, -1)
            Lmat = jnp.exp(segsum(ac))
            y_diag = jnp.einsum('bclhn,bcshn,bhcls,bcshp->bclhp', Cc, Bc, Lmat, uc)
            decay_states = jnp.exp(a_cum[..., -1:] - a_cum)
            states = jnp.einsum('bclhn,bhcl,bclhp->bchpn', Bc, decay_states, uc)
            chunk_decay = jnp.exp(a_cum[..., -1])

            def step(s, inp):
                dec, st = inp
                return (s * dec[..., None, None] + st, s)
            xs = (jnp.moveaxis(chunk_decay, -1, 0), jnp.moveaxis(states, 1, 0))
            s0 = jnp.zeros((b, NHEADS, HEADDIM, DSTATE), xn.dtype)
            _, prev = lax.scan(step, s0, xs)
            prev = jnp.moveaxis(prev, 0, 1)
            y_off = jnp.einsum('bclhn,bchpn,bhcl->bclhp', Cc, prev, jnp.exp(a_cum))
            y = (y_diag + y_off).reshape(b, l, NHEADS, HEADDIM) + d_skip[:, None] * xh
            y = y.reshape(b, l, DINNER)
            g = rmsnorm(y * jax.nn.silu(z), EPS_GATE) * norm_w
            return g @ w_out
        key = jax.random.key(seed)
        ks = jax.random.split(key, 10)
        sc = lambda k, sh, s: jax.random.normal(k, sh, jnp.float32) * s
        return {'x': sc(ks[0], (B, L, D), 1.0), 'w_in': sc(ks[1], (D, DINPROJ), D ** (-0.5)), 'conv_w': sc(ks[2], (CONVDIM, DCONV), DCONV ** (-0.5)), 'conv_b': jnp.zeros((CONVDIM,), jnp.float32), 'dt_bias': sc(ks[3], (NHEADS,), 0.5), 'a_log': jnp.log(jax.random.uniform(ks[4], (NHEADS,), jnp.float32, 1.0, 16.0)), 'd_skip': jnp.ones((NHEADS,), jnp.float32), 'norm_w': jnp.ones((DINNER,), jnp.float32), 'w_out': sc(ks[5], (DINNER, D), DINNER ** (-0.5)), 'w_fc': sc(ks[6], (D, 4 * D), D ** (-0.5)), 'w_proj': sc(ks[7], (4 * D, D), (4 * D) ** (-0.5))}
    _L0_attn_in = _L0_attn_setup()

    def _L0_ffn_setup():
        import jax, jax.numpy as jnp
        import numpy as np
        D_IN, D_HID = (256, 1024)

        def _ternary(key, shape):
            return jax.random.randint(key, shape, -1, 2).astype(jnp.float32)

        def _tlin(x, w, s):
            return jnp.einsum('bsi,oi->bso', x, w) * s
        key = jax.random.key(seed)
        ks = jax.random.split(key, 12)
        inv = lambda fan: 1.0 / np.sqrt(fan).astype(np.float32)
        return {'x': jax.random.normal(ks[0], (4, 512, D_IN), dtype=jnp.float32), 'w1_w': _ternary(ks[1], (D_HID, D_IN)), 'w1_s': jax.random.uniform(ks[2], (D_HID,), dtype=jnp.float32) * inv(D_IN), 'w2_w': _ternary(ks[3], (D_HID, D_IN)), 'w2_s': jax.random.uniform(ks[4], (D_HID,), dtype=jnp.float32) * inv(D_IN), 'h1_w': _ternary(ks[5], (D_HID, D_HID)), 'h1_s': jax.random.uniform(ks[6], (D_HID,), dtype=jnp.float32) * inv(D_HID), 'h2_w': _ternary(ks[7], (D_HID, D_HID)), 'h2_s': jax.random.uniform(ks[8], (D_HID,), dtype=jnp.float32) * inv(D_HID), 'w3_w': _ternary(ks[9], (D_IN, D_HID)), 'w3_s': jax.random.uniform(ks[10], (D_IN,), dtype=jnp.float32) * inv(D_HID)}
    _L0_ffn_in = _L0_ffn_setup()
    _d = {'L0_attn_x': _L0_attn_in['x'], 'L0_attn_w_in': _L0_attn_in['w_in'], 'L0_attn_conv_w': _L0_attn_in['conv_w'], 'L0_attn_conv_b': _L0_attn_in['conv_b'], 'L0_attn_dt_bias': _L0_attn_in['dt_bias'], 'L0_attn_a_log': _L0_attn_in['a_log'], 'L0_attn_d_skip': _L0_attn_in['d_skip'], 'L0_attn_norm_w': _L0_attn_in['norm_w'], 'L0_attn_w_out': _L0_attn_in['w_out'], 'L0_attn_w_fc': _L0_attn_in['w_fc'], 'L0_attn_w_proj': _L0_attn_in['w_proj'], 'L0_ffn_w1_w': _L0_ffn_in['w1_w'], 'L0_ffn_w1_s': _L0_ffn_in['w1_s'], 'L0_ffn_w2_w': _L0_ffn_in['w2_w'], 'L0_ffn_w2_s': _L0_ffn_in['w2_s'], 'L0_ffn_h1_w': _L0_ffn_in['h1_w'], 'L0_ffn_h1_s': _L0_ffn_in['h1_s'], 'L0_ffn_h2_w': _L0_ffn_in['h2_w'], 'L0_ffn_h2_s': _L0_ffn_in['h2_s'], 'L0_ffn_w3_w': _L0_ffn_in['w3_w'], 'L0_ffn_w3_s': _L0_ffn_in['w3_s']}
    _x0 = _d['L0_attn_x']
    _d['L0_attn_x'] = jax.random.normal(jax.random.fold_in(jax.random.key(seed), 1), (2, 2048, 256), dtype=_x0.dtype)
    del _x0
    return _d

def reference(L0_attn_x, L0_attn_w_in, L0_attn_conv_w, L0_attn_conv_b, L0_attn_dt_bias, L0_attn_a_log, L0_attn_d_skip, L0_attn_norm_w, L0_attn_w_out, L0_attn_w_fc, L0_attn_w_proj, L0_ffn_w1_w, L0_ffn_w1_s, L0_ffn_w2_w, L0_ffn_w2_s, L0_ffn_h1_w, L0_ffn_h1_s, L0_ffn_h2_w, L0_ffn_h2_s, L0_ffn_w3_w, L0_ffn_w3_s):

    def _L0_attn_ref(x, w_in, conv_w, conv_b, dt_bias, a_log, d_skip, norm_w, w_out, w_fc, w_proj):
        import jax, jax.numpy as jnp
        import numpy as np
        from jax import lax
        B, L, D = (4, 512, 256)
        DSTATE, DCONV, EXPAND, NGROUPS, CHUNK = (128, 4, 2, 1, 64)
        HEADDIM = 64
        DINNER = EXPAND * D
        NHEADS = DINNER // HEADDIM
        CONVDIM = DINNER + 2 * NGROUPS * DSTATE
        DINPROJ = 2 * DINNER + 2 * NGROUPS * DSTATE + NHEADS
        EPS_OUT = 1.1920929e-07
        EPS_GATE = 1e-05

        def rmsnorm(x, eps):
            return x * lax.rsqrt(jnp.mean(x * x, -1, keepdims=True) + eps)

        def segsum(x):
            c = x.shape[-1]
            xc = jnp.cumsum(x, -1)
            d = xc[..., :, None] - xc[..., None, :]
            mask = jnp.tril(jnp.ones((c, c), bool))
            return jnp.where(mask, d, -jnp.inf)

        def mamba2(xn, w_in, conv_w, conv_b, dt_bias, a_log, d_skip, norm_w, w_out):
            b, l, _ = xn.shape
            zxbcdt = xn @ w_in
            z = zxbcdt[..., :DINNER]
            xbc = zxbcdt[..., DINNER:DINNER + CONVDIM]
            dt_raw = zxbcdt[..., DINNER + CONVDIM:]
            xp = jnp.pad(xbc, ((0, 0), (DCONV - 1, 0), (0, 0)))
            xc = sum((xp[:, k:k + l, :] * conv_w[:, k] for k in range(DCONV))) + conv_b
            xc = jax.nn.silu(xc)
            xh = xc[..., :DINNER].reshape(b, l, NHEADS, HEADDIM)
            Bm = xc[..., DINNER:DINNER + NGROUPS * DSTATE].reshape(b, l, NGROUPS, DSTATE)
            Cm = xc[..., DINNER + NGROUPS * DSTATE:].reshape(b, l, NGROUPS, DSTATE)
            hpg = NHEADS // NGROUPS
            Bh = jnp.repeat(Bm, hpg, 2)
            Ch = jnp.repeat(Cm, hpg, 2)
            dt = jax.nn.softplus(dt_raw + dt_bias)
            a = dt * -jnp.exp(a_log)
            u = dt[..., None] * xh
            nc = l // CHUNK
            uc = u.reshape(b, nc, CHUNK, NHEADS, HEADDIM)
            Bc = Bh.reshape(b, nc, CHUNK, NHEADS, DSTATE)
            Cc = Ch.reshape(b, nc, CHUNK, NHEADS, DSTATE)
            ac = a.reshape(b, nc, CHUNK, NHEADS).transpose(0, 3, 1, 2)
            a_cum = jnp.cumsum(ac, -1)
            Lmat = jnp.exp(segsum(ac))
            y_diag = jnp.einsum('bclhn,bcshn,bhcls,bcshp->bclhp', Cc, Bc, Lmat, uc)
            decay_states = jnp.exp(a_cum[..., -1:] - a_cum)
            states = jnp.einsum('bclhn,bhcl,bclhp->bchpn', Bc, decay_states, uc)
            chunk_decay = jnp.exp(a_cum[..., -1])

            def step(s, inp):
                dec, st = inp
                return (s * dec[..., None, None] + st, s)
            xs = (jnp.moveaxis(chunk_decay, -1, 0), jnp.moveaxis(states, 1, 0))
            s0 = jnp.zeros((b, NHEADS, HEADDIM, DSTATE), xn.dtype)
            _, prev = lax.scan(step, s0, xs)
            prev = jnp.moveaxis(prev, 0, 1)
            y_off = jnp.einsum('bclhn,bchpn,bhcl->bclhp', Cc, prev, jnp.exp(a_cum))
            y = (y_diag + y_off).reshape(b, l, NHEADS, HEADDIM) + d_skip[:, None] * xh
            y = y.reshape(b, l, DINNER)
            g = rmsnorm(y * jax.nn.silu(z), EPS_GATE) * norm_w
            return g @ w_out
        h = x + mamba2(rmsnorm(x, EPS_OUT), w_in, conv_w, conv_b, dt_bias, a_log, d_skip, norm_w, w_out)
        m = rmsnorm(h, EPS_OUT) @ w_fc
        m = jnp.square(jax.nn.relu(m)) @ w_proj
        return h + m

    def _L0_ffn_ref(x, w1_w, w1_s, w2_w, w2_s, h1_w, h1_s, h2_w, h2_s, w3_w, w3_s):
        import jax, jax.numpy as jnp
        import numpy as np
        D_IN, D_HID = (256, 1024)

        def _ternary(key, shape):
            return jax.random.randint(key, shape, -1, 2).astype(jnp.float32)

        def _tlin(x, w, s):
            return jnp.einsum('bsi,oi->bso', x, w) * s
        h = jax.nn.silu(_tlin(x, w1_w, w1_s)) * _tlin(x, w2_w, w2_s)
        h = jax.nn.gelu(_tlin(h, h1_w, h1_s), approximate=False)
        h = jax.nn.gelu(_tlin(h, h2_w, h2_s), approximate=False)
        return _tlin(h, w3_w, w3_s)
    x = L0_attn_x
    x = _layernorm(x + _L0_attn_ref(x, L0_attn_w_in, L0_attn_conv_w, L0_attn_conv_b, L0_attn_dt_bias, L0_attn_a_log, L0_attn_d_skip, L0_attn_norm_w, L0_attn_w_out, L0_attn_w_fc, L0_attn_w_proj), axis=-1)
    x = _layernorm(x + _L0_ffn_ref(x, L0_ffn_w1_w, L0_ffn_w1_s, L0_ffn_w2_w, L0_ffn_w2_s, L0_ffn_h1_w, L0_ffn_h1_s, L0_ffn_h2_w, L0_ffn_h2_s, L0_ffn_w3_w, L0_ffn_w3_s), axis=-1)
    return x

_drawn_inputs = setup_inputs


def setup_inputs(seed=0):
    import zlib

    import numpy as np

    out = dict(_drawn_inputs(seed))
    spreads = {'L0_attn_conv_b': (0.0, 0.1), 'L0_attn_d_skip': (1.0, 0.2), 'L0_attn_norm_w': (1.0, 0.2)}
    factors = {'L0_ffn_w1_w': 8.0,
     'L0_ffn_w1_s': 8.0,
     'L0_ffn_w2_w': 8.0,
     'L0_ffn_w2_s': 8.0,
     'L0_ffn_h1_w': 8.0,
     'L0_ffn_h1_s': 8.0,
     'L0_ffn_h2_w': 8.0,
     'L0_ffn_h2_s': 8.0,
     'L0_ffn_w3_w': 8.0,
     'L0_ffn_w3_s': 8.0}
    for name, (base, spread) in spreads.items():
        noise = np.random.default_rng([zlib.crc32(name.encode()), seed]).standard_normal(out[name].shape)
        drawn = base * np.exp(spread * noise) if base else spread * noise
        out[name] = jnp.asarray(drawn.astype(out[name].dtype))
    for name, factor in factors.items():
        out[name] = (out[name] * factor).astype(out[name].dtype)
    return out
```

```python
from contextlib import ExitStack

import concourse.bass as bass
from concourse import mybir

F32 = mybir.dt.float32
F32R = mybir.dt.float32r
I32 = mybir.dt.int32
ALU = mybir.AluOpType
ACT = mybir.ActivationFunctionType
AX = mybir.AxisListType

P = 128
TILE = 512
CH = TILE // P
D = 256
KD = D // P
INNER = 512
KI = INNER // P
HEADS = 8
HDIM = INNER // HEADS
CONV = INNER + 2 * P
MC = CONV // P
TAPS = 4
HALO = TAPS - 1
PROJ = 2 * INNER + 2 * P + HEADS
HID = 4 * D
KH = HID // P
EPS_OUT = 1.1920929e-07
EPS_GATE = 1e-05
EPS_LN = 1e-05
LOW_BITS = 0xFFF

ACT_ITEMS = ([f"xbc{m}" for m in (4, 5, 0, 1, 2, 3)] + ["dt"] + [f"z{c}" for c in range(CH)] + ["cums"]
             + [f"{n}{c}" for c in range(CH) for n in ("xt", "dlo", "dhi")] + [f"fc{j}" for j in range(KH)])
DVE_ITEMS = ["xnT0", "xnT1", "gb0"]
for _c in range(CH):
    DVE_ITEMS += [f"gb{_c + 1}"] * (_c < CH - 1) + [f"yoff{_c}", f"ydiag{_c}"]
    DVE_ITEMS += [f"yT{_c - 1}", f"wo{_c - 1}"] * (_c > 0)
DVE_ITEMS += [f"yT{CH - 1}", f"wo{CH - 1}", "hT0", "hT1"]
ACT_BANKS, DVE_BANKS = 2, 3
AI = {n: i for i, n in enumerate(ACT_ITEMS)}
DI = {n: i for i, n in enumerate(DVE_ITEMS)}
NA, ND = len(ACT_ITEMS), len(DVE_ITEMS)
assert NA % ACT_BANKS == 0 and ND % DVE_BANKS == 0
CONV_ORDER = (4, 5, 0, 1, 2, 3)

B_ACT_BANKS, B_DVE_BANKS = 4, 2
NBA, NBD = 3 * KH, KD + KH


def post_ln_block(nc, x, w_in, conv_w, conv_b, dt_bias, a_log, d_skip, norm_w, w_out, w_fc, w_proj,
                  w1, s1, w2, s2, h1, sh1, h2, sh2, w3, s3, out, seq_len):
    N = x.shape[0]
    TILES = N // TILE
    SEQ_TILES = seq_len // TILE
    SEQS = TILES // SEQ_TILES

    ctx = ExitStack()
    with ctx:
        def sb(name, shape, dt=F32, into=ctx):
            return into.enter_context(nc.sbuf_tensor(name, shape, dt))

        def sem(name):
            return ctx.enter_context(nc.semaphore(name))

        class Steps:

            def __init__(self, eng, s, base):
                self.eng, self.s, self.base, self.n = eng, s, base, 0

            def mark(self, ins):
                self.n += 1
                ins.then_inc(self.s, 1)
                return self.n

            def wait(self, n):
                self.eng.wait_ge(self.s, self.base + n)

            def link(self, ins):
                self.wait(self.mark(ins))

        def row_stats(nc, step, src, bn, mv, last):
            for c in range(CH):
                step.mark(nc.vector.bn_stats(bn[:, c, :], src[:, c, :]))
            step.wait(step.n)
            tt = nc.vector.tensor_tensor
            step.mark(tt(mv[:, 0, :], bn[:, :, 1], bn[:, :, 4], ALU.add))
            step.mark(tt(mv[:, 2, :], bn[:, :, 1], bn[:, :, 4], ALU.subtract))
            step.link(tt(mv[:, 1, :], bn[:, :, 2], bn[:, :, 5], ALU.add))
            step.mark(nc.vector.tensor_scalar(mv[:, 0, :], mv[:, 0, :], 0.5, None, ALU.mult))
            step.link(tt(mv[:, 2, :], mv[:, 2, :], mv[:, 2, :], ALU.mult))
            last(nc.vector.scalar_tensor_tensor(out=mv[:, 1, :], in0=mv[:, 2, :], scalar=D / 4.0, in1=mv[:, 1, :],
                                                op0=ALU.mult, op1=ALU.add))

        STAT_STEPS = CH + 5
        rows = lambda ap, at: (ap.rearrange("n f -> (n f)")[bass.ds(at, TILE * D)]
                               .rearrange("(c p f) -> p c f", p=P, f=D))

        banks = [ctx.enter_context(nc.psum_tensor(f"bank{i}", [P, 512], F32)) for i in range(8)]

        raw = {}
        for name, src in (("w1", w1), ("w2", w2), ("h1", h1), ("h2", h2), ("w3", w3)):
            raw[name] = nc.dram_tensor(f"{name}_raw", src.shape, F32, kind="Internal").ap()
        x1_dram = nc.dram_tensor("x1_rows", (N, D), F32, kind="Internal").ap()

        ident = sb("ident", [P, P])
        ones = sb("ones", [P, P])
        zero = sb("zero", [P, 1])
        eps = sb("eps", [P, 4])
        w1_sb = sb("w1_sb", [P, KD, HID], F32R)
        w2_sb = sb("w2_sb", [P, KD, HID], F32R)

        s_raw = sem("raw_copied")
        s_w12 = sem("w12_loaded")
        s_params = sem("params_loaded")
        s_masks = sem("masks_ready")
        s_stage = [sem(f"{n}_staged") for n in ("w_in", "w_out", "w_fc", "w_proj")]
        s_nw = sem("w_out_scaled")
        s_whi = sem("weight_hi_ready")
        s_wlo = sem("weight_lo_ready")
        s_nega = sem("neg_a_ready")
        s_zero = sem("state_cleared")
        s_hz = sem("halo_cleared")

        a_ctx = ctx.enter_context(ExitStack())
        A = lambda name, shape, dt=F32: sb(name, shape, dt, a_ctx)
        tri_le = A("tri_le", [P, P])
        tri_gt = A("tri_gt", [P, P])
        w_in_hi, w_in_lo = A("w_in_hi", [P, KD, PROJ], F32R), A("w_in_lo", [P, KD, PROJ], F32R)
        w_out_hi, w_out_lo = A("w_out_hi", [P, KI, D], F32R), A("w_out_lo", [P, KI, D], F32R)
        w_fc_hi, w_fc_lo = A("w_fc_hi", [P, KD, HID], F32R), A("w_fc_lo", [P, KD, HID], F32R)
        w_pj_hi, w_pj_lo = A("w_pj_hi", [P, KH, D], F32R), A("w_pj_lo", [P, KH, D], F32R)
        conv_w_sb, conv_b_sb = A("conv_w_sb", [P, MC, TAPS]), A("conv_b_sb", [P, MC])
        dt_bias_b, neg_a, dskip_b = A("dt_bias_b", [P, HEADS]), A("neg_a", [P, HEADS]), A("dskip_b", [P, HEADS])

        with ExitStack() as w_ctx, nc.Block() as block:
            W = lambda name, shape: sb(name, shape, F32, w_ctx)
            st_in, st_out = W("st_in", [P, KD, PROJ]), W("st_out", [P, KI, D])
            st_fc, st_pj = W("st_fc", [P, KD, HID]), W("st_pj", [P, KH, D])
            norm_w_sb = W("norm_w_sb", [P, KI])
            a_log_b = W("a_log_b", [P, HEADS])
            splits = [(st_in, w_in_hi, w_in_lo), (st_out, w_out_hi, w_out_lo),
                      (st_fc, w_fc_hi, w_fc_lo), (st_pj, w_pj_hi, w_pj_lo)]

            @block.sync
            def _(sp):
                sp.dma_start(a_log_b[:], a_log.partition_broadcast(P)).then_inc(s_params, 16)
                sp.dma_start(dt_bias_b[:], dt_bias.partition_broadcast(P)).then_inc(s_params, 16)
                sp.dma_start(dskip_b[:], d_skip.partition_broadcast(P)).then_inc(s_params, 16)
                sp.dma_start(norm_w_sb[:], norm_w).then_inc(s_params, 16)
                sp.dma_start(conv_w_sb[:], conv_w).then_inc(s_params, 16)
                sp.dma_start(conv_b_sb[:], conv_b).then_inc(s_params, 16)
                sp.dma_start(st_in[:], w_in.rearrange("(k p) n -> p k n", p=P)).then_inc(s_stage[0], 16)
                sp.dma_start(st_out[:], w_out.rearrange("(k p) n -> p k n", p=P)).then_inc(s_stage[1], 16)
                sp.dma_start(st_fc[:], w_fc.rearrange("(k p) n -> p k n", p=P)).then_inc(s_stage[2], 16)
                sp.dma_start(st_pj[:], w_proj.rearrange("(k p) n -> p k n", p=P)).then_inc(s_stage[3], 16)
                for s in s_stage:
                    sp.wait_ge(s, 16)
                for n, (name, src) in enumerate((("w1", w1), ("w2", w2), ("h1", h1), ("h2", h2), ("w3", w3))):
                    sp.dma_start(raw[name], src).then_inc(s_raw, 16)
                    if n == 1:
                        sp.wait_ge(s_raw, 32)
                        for name2, dst in (("w1", w1_sb), ("w2", w2_sb)):
                            sp.dma_start(dst[:].bitcast(F32),
                                         raw[name2].rearrange("(k p) n -> p k n", p=P)).then_inc(s_w12, 16)

            @block.gpsimd
            def _(pool):
                pool.memset(ident[:], 0.0).then_inc(s_masks, 1)
                pool.memset(ones[:], 1.0).then_inc(s_masks, 1)
                for i, v in enumerate((EPS_OUT, EPS_GATE, EPS_LN, 1.0)):
                    pool.memset(eps[:, i:i + 1], v).then_inc(s_masks, 1)
                pool.memset(zero[:], 0.0).then_inc(s_masks, 1)
                pool.wait_ge(s_masks, 7)
                pool.affine_select(out=ident[:], in_=ident[:], compare_op=ALU.not_equal, fill=1.0, base=0,
                                   pattern=[[-1, P]], channel_multiplier=1).then_inc(s_masks, 1)
                pool.affine_select(out=tri_le[:], in_=ones[:], compare_op=ALU.is_ge, fill=0.0, base=0,
                                   pattern=[[1, P]], channel_multiplier=-1).then_inc(s_masks, 1)
                pool.affine_select(out=tri_gt[:], in_=ones[:], compare_op=ALU.is_gt, fill=0.0, base=0,
                                   pattern=[[-1, P]], channel_multiplier=1).then_inc(s_masks, 1)

            @block.scalar
            def _(act):
                act.wait_ge(s_params, 96)
                nc.scalar.activation(neg_a[:], a_log_b[:], ACT.Exp).then_inc(s_nega, 1)
                for n, (st, hi, lo) in enumerate(splits):
                    act.wait_ge(s_stage[n], 16)
                    if st is st_out:
                        act.wait_ge(s_nw, KI)
                    nc.scalar.activation(hi[:], st[:], ACT.Copy).then_inc(s_whi, 1)

            @block.vector
            def _(dve):
                dve.wait_ge(s_params, 96)
                dve.wait_ge(s_stage[1], 16)
                for k in range(KI):
                    nc.vector.tensor_scalar(st_out[:, k, :], st_out[:, k, :], norm_w_sb[:, k:k + 1], None,
                                            ALU.mult).then_inc(s_nw, 1)
                dve.wait_ge(s_nega, 1)
                nc.vector.tensor_scalar(neg_a[:], neg_a[:], -1.0, None, ALU.mult).then_inc(s_nega, 1)
                dve.wait_ge(s_nw, KI)
                for n, (st, hi, lo) in enumerate(splits):
                    dve.wait_ge(s_whi, n + 1)
                    nc.vector.tensor_tensor(lo[:], st[:], hi[:].bitcast(F32), ALU.subtract).then_inc(s_wlo, 1)

        x_in, x_res = A("x_in", [P, CH, D]), A("x_res", [P, CH, D])
        junk = A("junk", [P, INNER])
        xn = A("xn", [P, CH, D])
        xnT_hi, xnT_lo = A("xnT_hi", [P, KD, TILE], F32R), A("xnT_lo", [P, KD, TILE], F32R)
        xp = A("xp", [P, MC, HALO + TILE])
        xc = A("xc", [P, MC, TILE])
        z_s = A("z_s", [P, CH, INNER])
        sm = A("sm", [P, 16, CH * HEADS])
        dt_raw, v_dt, ab_dt, e_dt, ln_dt, c_dt, r_dt, l_dt, dt, a = (sm[:, i, :] for i in range(10))
        dec = A("dec", [P, 3, CH * HEADS])
        st = A("st", [P, 8, CH])
        ssx, lnx, rsx, ssy, lny, rsy, ssh, lnh = (st[:, i, :] for i in range(8))
        st2 = A("st2", [P, 4, CH])
        rsh, r2h, lnv, rsv = (st2[:, i, :] for i in range(4))
        bn = A("bn", [P, CH, 6])
        mv = A("mv", [P, 3, CH])
        RA = A("RA", [P, 2, HEADS, P])
        E = A("E", [P, 2, HEADS, P])
        Gm, Bt = A("Gm", [P, 2, P]), A("Bt", [P, 2, P])
        xt, u, ud, y = (A(n, [P, 2, INNER]) for n in ("xt", "u", "ud", "y"))
        S = A("S", [P, 2, INNER])
        tmp = A("tmp", [P, INNER])
        yT_hi, yT_lo = A("yT_hi", [P, KI, P], F32R), A("yT_lo", [P, KI, P], F32R)
        h = A("h", [P, CH, D])
        hT_hi, hT_lo = A("hT_hi", [P, KD, TILE], F32R), A("hT_lo", [P, KD, TILE], F32R)
        m_fc = A("m_fc", [P, 2, TILE])
        m_hi, m_lo = A("m_hi", [P, 2, TILE], F32R), A("m_lo", [P, 2, TILE], F32R)
        x1 = A("x1", [P, CH, D])

        act_bank = lambda i: banks[i % ACT_BANKS]
        dve_bank = lambda i: banks[ACT_BANKS + i % DVE_BANKS]
        st_bank = banks[5]
        pj_banks = banks[6:8]

        s_x = sem("x_loaded")
        s_xres = sem("x_kept")
        s_rsx = sem("x_rstd_ready")
        s_xn = sem("xn_ready")
        s_ai = sem("act_item_ready")
        s_ad = sem("act_item_drained")
        s_di = sem("dve_item_ready")
        s_dd = sem("dve_item_drained")
        s_hi = sem("activation_hi_ready")
        s_dtl = sem("dt_log_ready")
        s_dtv = sem("dt_biased")
        s_a = sem("a_ready")
        s_cv = sem("conv_ready")
        s_xc = sem("xc_ready")
        s_halo = sem("halo_kept")
        s_ra = sem("masked_a_ready")
        s_M = sem("decayed_scores_ready")
        s_u = sem("u_ready")
        s_sdec = sem("state_decayed")
        s_si = sem("state_item_ready")
        s_sup = sem("state_updated")
        s_y = sem("y_ready")
        s_rsy = sem("y_rstd_ready")
        s_rsh = sem("h_rstd_ready")
        s_m = sem("m_ready")
        s_mh = sem("m_hi_ready")
        s_ml = sem("m_lo_ready")
        s_pj = sem("proj_ready")
        s_pjd = sem("proj_drained")
        s_mv = sem("ln_var_ready")
        s_rsv = sem("ln_rstd_ready")
        s_x1 = sem("x1_ready")
        s_x1o = sem("x1_stored")
        s_as = sem("act_step")
        s_ds = sem("dve_step")

        with nc.Block() as block:
            @block.sync
            def _(sp):
                def load(it, at):
                    sp.wait_ge(s_xn, CH * it)
                    sp.dma_start(x_in[:], rows(x, at)).then_inc(s_x, 16)

                def store(it, at):
                    sp.wait_ge(s_x1, CH * it + CH)
                    sp.dma_start(rows(x1_dram, at), x1[:]).then_inc(s_x1o, 16)

                load(0, 0)
                with sp.Fori(0, TILES - 1) as it:
                    at, at_next = sp.snap(it * (TILE * D)), sp.snap((it + 1) * (TILE * D))
                    load(it + 1, at_next)
                    store(it, at)
                store(TILES - 1, (N - TILE) * D)
                sp.wait_ge(s_x1o, 16 * TILES)
                sp.wait_ge(s_w12, 32)
                sp.wait_ge(s_raw, 80)

            @block.tensor
            def _(pe):
                def three(o, hi, lo, rhi, rlo, first, last):
                    pe.matmul(o, lo, rhi, start=first, stop=False, skip_group_check=True)
                    pe.matmul(o, hi, rlo, start=False, stop=False, skip_group_check=True)
                    return pe.matmul(o, hi, rhi, start=False, stop=last, skip_group_check=True)

                def tile(it):
                    def act_item(name):
                        i = AI[name]
                        pe.wait_ge(s_ad, NA * it + i + 1)
                        return act_bank(i)

                    def dve_item(name):
                        i = DI[name]
                        pe.wait_ge(s_dd, ND * it + i + 1)
                        return dve_bank(i)

                    pe.wait_ge(s_xn, CH * it + CH)
                    for k in range(KD):
                        b = dve_item(f"xnT{k}")
                        for c in range(CH):
                            last = pe.transpose(b[:, c * P:(c + 1) * P], xn[:, c, k * P:(k + 1) * P], ident[:])
                        last.then_inc(s_di, 1)
                    pe.wait_ge(s_dd, ND * it + DI["xnT1"] + 1 + DVE_BANKS)

                    for m in CONV_ORDER:
                        b = act_item(f"xbc{m}")
                        cols = slice(INNER + m * P, INNER + (m + 1) * P)
                        for k in range(KD):
                            last = three(b[:], w_in_hi[:, k, cols], w_in_lo[:, k, cols],
                                         xnT_hi[:, k, :], xnT_lo[:, k, :], k == 0, k == KD - 1)
                        last.then_inc(s_ai, 1)
                    b = act_item("dt")
                    cols = slice(PROJ - HEADS, PROJ)
                    for c in range(CH):
                        tok = slice(c * P, (c + 1) * P)
                        for k in range(KD):
                            last = three(b[:, c * HEADS:(c + 1) * HEADS], xnT_hi[:, k, tok], xnT_lo[:, k, tok],
                                         w_in_hi[:, k, cols], w_in_lo[:, k, cols], k == 0, k == KD - 1)
                    last.then_inc(s_ai, 1)
                    for c in range(CH):
                        b = act_item(f"z{c}")
                        tok = slice(c * P, (c + 1) * P)
                        for k in range(KD):
                            last = three(b[:], xnT_hi[:, k, tok], xnT_lo[:, k, tok],
                                         w_in_hi[:, k, 0:INNER], w_in_lo[:, k, 0:INNER], k == 0, k == KD - 1)
                        last.then_inc(s_ai, 1)
                    b = act_item("cums")
                    pe.wait_ge(s_a, it + 1)
                    for i, tri in enumerate((tri_le, tri_gt, ones)):
                        last = pe.matmul(b[:, i * CH * HEADS:(i + 1) * CH * HEADS], tri[:], a, start=True, stop=True)
                    last.then_inc(s_ai, 1)

                    def pre(c):
                        tok = slice(c * P, (c + 1) * P)
                        b = act_item(f"xt{c}")
                        pe.wait_ge(s_xc, MC * it + MC)
                        for m in range(KI):
                            last = pe.transpose(b[:, m * P:(m + 1) * P], xc[:, m, tok], ident[:])
                        last.then_inc(s_ai, 1)
                        b = dve_item(f"gb{c}")
                        pe.transpose(b[:, P:2 * P], xc[:, KI, tok], ident[:])
                        pe.matmul(b[:, 0:P], xc[:, KI, tok], xc[:, KI + 1, tok], start=True, stop=True,
                                  skip_group_check=True).then_inc(s_di, 1)
                        for half, name in enumerate(("dlo", "dhi")):
                            b = act_item(f"{name}{c}")
                            pe.wait_ge(s_ra, CH * it + c + 1)
                            pe.matmul(b[:], tri_gt[:], RA[:, c % 2, half * 4:half * 4 + 4, :].rearrange("p h l -> p (h l)"),
                                      start=True, stop=True).then_inc(s_ai, 1)

                    def main(c):
                        tok = slice(c * P, (c + 1) * P)
                        b = dve_item(f"yoff{c}")
                        pe.wait_ge(s_sdec, CH * it + c + 1)
                        pe.matmul(b[:], xc[:, KI + 1, tok], S[:, c % 2, :], start=True, stop=True).then_inc(s_di, 1)
                        b = dve_item(f"ydiag{c}")
                        pe.wait_ge(s_M, CH * it + c + 1)
                        pe.wait_ge(s_u, 3 * (CH * it + c) + 2)
                        for i in range(HEADS):
                            hs = slice(i * HDIM, (i + 1) * HDIM)
                            last = pe.matmul(b[:, hs], E[:, c % 2, i, :], u[:, c % 2, hs], start=True, stop=True)
                        last.then_inc(s_di, 1)
                        pe.wait_ge(s_sup, CH * it + c)
                        pe.matmul(st_bank[:], Bt[:, c % 2, :], ud[:, c % 2, :], start=True, stop=True).then_inc(s_si, 1)

                    def tail(c):
                        b = dve_item(f"yT{c}")
                        pe.wait_ge(s_y, CH * it + c + 1)
                        for k in range(KI):
                            last = pe.transpose(b[:, k * P:(k + 1) * P], y[:, c % 2, k * P:(k + 1) * P], ident[:])
                        last.then_inc(s_di, 1)
                        b = dve_item(f"wo{c}")
                        pe.wait_ge(s_dd, ND * it + DI[f"yT{c}"] + 1 + DVE_BANKS)
                        for k in range(KI):
                            last = three(b[:, 0:D], yT_hi[:, k, :], yT_lo[:, k, :],
                                         w_out_hi[:, k, :], w_out_lo[:, k, :], k == 0, k == KI - 1)
                        last.then_inc(s_di, 1)

                    pre(0)
                    for c in range(CH):
                        if c < CH - 1:
                            pre(c + 1)
                        main(c)
                        if c > 0:
                            tail(c - 1)
                    tail(CH - 1)
                    for k in range(KD):
                        b = dve_item(f"hT{k}")
                        pe.wait_ge(s_dd, ND * it + DI[f"wo{CH - 1}"] + 1 + DVE_BANKS)
                        for c in range(CH):
                            last = pe.transpose(b[:, c * P:(c + 1) * P], h[:, c, k * P:(k + 1) * P], ident[:])
                        last.then_inc(s_di, 1)
                    pe.wait_ge(s_dd, ND * it + ND + DVE_BANKS)

                    def proj(j):
                        pe.wait_ge(s_ml, KH * it + j + 1)
                        if j == 0:
                            pe.wait_ge(s_pjd, CH * it)
                        for c in range(CH):
                            tok = slice(c * P, (c + 1) * P)
                            o = pj_banks[c // 2][:, (c % 2) * D:(c % 2 + 1) * D]
                            last = three(o, m_hi[:, j % 2, tok], m_lo[:, j % 2, tok], w_pj_hi[:, j, :],
                                         w_pj_lo[:, j, :], j == 0 and c % 2 == 0, j == KH - 1)
                        last.then_inc(s_pj, 1)

                    for j in range(KH):
                        b = act_item(f"fc{j}")
                        cols = slice(j * P, (j + 1) * P)
                        for k in range(KD):
                            last = three(b[:], w_fc_hi[:, k, cols], w_fc_lo[:, k, cols],
                                         hT_hi[:, k, :], hT_lo[:, k, :], k == 0, k == KD - 1)
                        last.then_inc(s_ai, 1)
                        if j > 0:
                            proj(j - 1)
                    proj(KH - 1)

                with pe.Fori(0, TILES) as it:
                    tile(it)

            @block.scalar
            def _(act):
                act.sem_inc(s_ad, ACT_BANKS)
                A_STEPS = 4 * CH + 5

                def tile(it):
                    step = Steps(act, s_as, A_STEPS * it)

                    def item(name):
                        act.wait_ge(s_ai, NA * it + AI[name] + 1)
                        return act_bank(AI[name])

                    def dve_hi(name, dst):
                        act.wait_ge(s_di, ND * it + DI[name] + 1)
                        nc.scalar.activation(dst, dve_bank(DI[name])[:], ACT.Copy).then_inc(s_hi, 1)

                    act.wait_ge(s_x, 16 * it + 16)
                    for c in range(CH):
                        step.link(nc.scalar.activation(junk[:, 0:D], x_in[:, c, :], ACT.Square,
                                                       accum_out=ssx[:, c:c + 1]))
                    step.link(nc.scalar.activation(lnx, ssx, ACT.Ln, scale=1.0 / D, bias=eps[:, 0:1]))
                    nc.scalar.activation(rsx, lnx, ACT.Exp, scale=-0.5).then_inc(s_rsx, 1)
                    for k in range(KD):
                        dve_hi(f"xnT{k}", xnT_hi[:, k, :])
                    act.wait_ge(s_halo, it)
                    for m in CONV_ORDER:
                        b = item(f"xbc{m}")
                        nc.scalar.activation(xp[:, m, HALO:], b[:], ACT.Copy).then_inc(s_ad, 1)
                    b = item("dt")
                    nc.scalar.activation(dt_raw, b[:, 0:CH * HEADS], ACT.Copy).then_inc(s_ad, 1)
                    act.wait_ge(s_dtv, it + 1)
                    step.link(nc.scalar.activation(ab_dt, v_dt, ACT.Abs))
                    step.link(nc.scalar.activation(e_dt, ab_dt, ACT.Exp, scale=-1.0))
                    nc.scalar.activation(ln_dt, e_dt, ACT.Ln, bias=eps[:, 3:4]).then_inc(s_dtl, 1)
                    act.wait_ge(s_y, CH * it)
                    for c in range(CH):
                        b = item(f"z{c}")
                        nc.scalar.activation(z_s[:, c, :], b[:], ACT.Silu).then_inc(s_ad, 1)
                    for n, m in enumerate(CONV_ORDER):
                        act.wait_ge(s_cv, MC * it + n + 1)
                        nc.scalar.activation(xc[:, m, :], xc[:, m, :], ACT.Silu,
                                             bias=conv_b_sb[:, m:m + 1]).then_inc(s_xc, 1)
                    b = item("cums")
                    act.wait_ge(s_sdec, CH * it)
                    nc.scalar.activation(dec[:].rearrange("p i n -> p (i n)"), b[:, 0:3 * CH * HEADS],
                                         ACT.Exp).then_inc(s_ad, 1)

                    def pre(c):
                        b = item(f"xt{c}")
                        if c >= 2:
                            act.wait_ge(s_u, 3 * (CH * it + c - 1))
                        nc.scalar.activation(xt[:, c % 2, :], b[:], ACT.Copy).then_inc(s_ad, 1)
                        for half, name in enumerate(("dlo", "dhi")):
                            b = item(f"{name}{c}")
                            if c >= 2:
                                act.wait_ge(s_di, ND * it + DI[f"ydiag{c - 2}"] + 1)
                            dst = E[:, c % 2, half * 4:half * 4 + 4, :].rearrange("p h l -> p (h l)")
                            nc.scalar.activation(dst, b[:], ACT.Exp).then_inc(s_ad, 1)

                    def gate_rms(c):
                        act.wait_ge(s_y, CH * it + c + 1)
                        step.link(nc.scalar.activation(junk[:], y[:, c % 2, :], ACT.Square,
                                                       accum_out=ssy[:, c:c + 1]))
                        step.link(nc.scalar.activation(lny[:, c:c + 1], ssy[:, c:c + 1], ACT.Ln,
                                                       scale=1.0 / INNER, bias=eps[:, 1:2]))
                        nc.scalar.activation(rsy[:, c:c + 1], lny[:, c:c + 1], ACT.Exp, scale=-0.5).then_inc(s_rsy, 1)

                    pre(0)
                    for c in range(CH):
                        if c < CH - 1:
                            pre(c + 1)
                        if c > 0:
                            gate_rms(c - 1)
                            dve_hi(f"yT{c - 1}", yT_hi[:].rearrange("p k n -> p (k n)"))
                    gate_rms(CH - 1)
                    dve_hi(f"yT{CH - 1}", yT_hi[:].rearrange("p k n -> p (k n)"))
                    act.wait_ge(s_dd, ND * it + DI[f"wo{CH - 1}"] + 1 + DVE_BANKS)
                    for c in range(CH):
                        step.link(nc.scalar.activation(junk[:, 0:D], h[:, c, :], ACT.Square,
                                                       accum_out=ssh[:, c:c + 1]))
                    step.link(nc.scalar.activation(lnh, ssh, ACT.Ln, scale=1.0 / D, bias=eps[:, 0:1]))
                    nc.scalar.activation(r2h, lnh, ACT.Exp, scale=-1.0).then_inc(s_rsh, 1)
                    for k in range(KD):
                        dve_hi(f"hT{k}", hT_hi[:, k, :])
                    for j in range(KH):
                        b = item(f"fc{j}")
                        if j >= 2:
                            act.wait_ge(s_ml, KH * it + j - 1)
                        m = m_fc[:, j % 2, :]
                        nc.scalar.activation(m, b[:], ACT.Relu).then_inc(s_ad, 1)
                        act.wait_ge(s_ad, NA * it + AI[f"fc{j}"] + 1 + ACT_BANKS)
                        nc.scalar.activation(m, m, ACT.Square).then_inc(s_m, 1)
                        if j >= 2:
                            act.wait_ge(s_pj, KH * it + j - 1)
                        act.wait_ge(s_m, KH * it + j + 1)
                        nc.scalar.activation(m_hi[:, j % 2, :], m_fc[:, j % 2, :], ACT.Copy).then_inc(s_mh, 1)
                    act.wait_ge(s_mv, it + 1)
                    step.link(nc.scalar.activation(lnv, mv[:, 1, :], ACT.Ln, scale=1.0 / D, bias=eps[:, 2:3]))
                    nc.scalar.activation(rsv, lnv, ACT.Exp, scale=-0.5).then_inc(s_rsv, 1)
                    return step.n

                with act.Fori(0, TILES) as it:
                    assert tile(it) == A_STEPS

            @block.gpsimd
            def _(pool):
                bc = lambda ap: ap.unsqueeze(2).broadcast_to([P, HEADS, HDIM])
                heads = lambda ap: ap.rearrange("p (h d) -> p h d", h=HEADS)
                with pool.Fori(0, SEQS) as seq:
                    pool.wait_ge(s_sup, CH * SEQ_TILES * seq)
                    pool.wait_ge(s_si, CH * SEQ_TILES * seq)
                    zeros = zero[:].broadcast_to([P, INNER])
                    nc.gpsimd.tensor_tensor(S[:, 0, :], zeros, zeros, ALU.add).then_inc(s_zero, 1)
                    with pool.Fori(0, SEQ_TILES) as j:
                        it = seq * SEQ_TILES + j

                        def masked_a(c):
                            if c >= 2:
                                pool.wait_ge(s_ai, NA * it + AI[f"dhi{c - 2}"] + 1)
                            nc.gpsimd.tensor_tensor(
                                RA[:, c % 2, :, :],
                                a[:, c * HEADS:(c + 1) * HEADS].unsqueeze(2).broadcast_to([P, HEADS, P]),
                                tri_le[:].unsqueeze(1).broadcast_to([P, HEADS, P]), ALU.mult).then_inc(s_ra, 1)

                        pool.wait_ge(s_a, it + 1)
                        masked_a(0)
                        for c in range(CH):
                            b, o = c % 2, 1 - c % 2
                            if c < CH - 1:
                                masked_a(c + 1)
                            hs = slice(c * HEADS, (c + 1) * HEADS)
                            pool.wait_ge(s_ad, NA * it + AI[f"xt{c}"] + 1 + ACT_BANKS)
                            if c >= 2:
                                pool.wait_ge(s_si, CH * it + c - 1)
                            nc.gpsimd.tensor_tensor(heads(u[:, b, :]), heads(xt[:, b, :]), bc(dt[:, hs]),
                                                    ALU.mult).then_inc(s_u, 1)
                            pool.wait_ge(s_u, 3 * (CH * it + c) + 1)
                            nc.gpsimd.tensor_tensor(heads(ud[:, b, :]), heads(u[:, b, :]), bc(dec[:, 1, hs]),
                                                    ALU.mult).then_inc(s_u, 1)
                            if c >= 2:
                                pool.wait_ge(s_rsy, CH * it + c - 1)
                                pool.wait_ge(s_di, ND * it + DI[f"yT{c - 2}"] + 1)
                            nc.gpsimd.tensor_tensor(heads(y[:, b, :]), heads(xt[:, b, :]), bc(dskip_b[:]),
                                                    ALU.mult).then_inc(s_u, 1)
                            pool.wait_ge(s_sup, CH * it + c)
                            pool.wait_ge(s_zero, seq + 1)
                            nc.gpsimd.tensor_tensor(heads(S[:, o, :]), heads(S[:, b, :]), bc(dec[:, 2, hs]),
                                                    ALU.mult).then_inc(s_sdec, 1)

            @block.vector
            def _(dve):
                dve.sem_inc(s_dd, DVE_BANKS)
                heads = lambda ap: ap.rearrange("p (h d) -> p h d", h=HEADS)

                def tile(it, seq):
                    step = Steps(dve, s_ds, D_STEPS * it)

                    def item(name):
                        dve.wait_ge(s_di, ND * it + DI[name] + 1)
                        return dve_bank(DI[name])

                    def lo_part(name, n_hi, hi, lo):
                        dve.wait_ge(s_hi, (2 * KD + CH) * it + n_hi)
                        nc.vector.tensor_tensor(lo, dve_bank(DI[name])[:], hi.bitcast(F32),
                                                ALU.subtract).then_inc(s_dd, 1)

                    dve.wait_ge(s_x, 16 * it + 16)
                    dve.wait_ge(s_x1, CH * it)
                    nc.vector.tensor_copy(x_res[:], x_in[:]).then_inc(s_xres, 1)
                    dve.wait_ge(s_rsx, it + 1)
                    for c in range(CH):
                        nc.vector.tensor_scalar(xn[:, c, :], x_in[:, c, :], rsx[:, c:c + 1], None,
                                                ALU.mult).then_inc(s_xn, 1)
                    for k in range(KD):
                        lo_part(f"xnT{k}", k + 1, xnT_hi[:, k, :], xnT_lo[:, k, :])

                    def taps(ms):
                        marks = {}
                        for t in range(TAPS):
                            for m in ms:
                                src = xp[:, m, t:t + TILE]
                                w = conv_w_sb[:, m, t:t + 1]
                                if t == 0:
                                    dve.wait_ge(s_ad, NA * it + AI[f"xbc{m}"] + 1 + ACT_BANKS)
                                    marks[m] = step.mark(nc.vector.tensor_scalar(xc[:, m, :], src, w, None, ALU.mult))
                                    continue
                                step.wait(marks[m])
                                ins = nc.vector.scalar_tensor_tensor(out=xc[:, m, :], in0=src, scalar=w,
                                                                     in1=xc[:, m, :], op0=ALU.mult, op1=ALU.add)
                                if t == TAPS - 1:
                                    ins.then_inc(s_cv, 1)
                                else:
                                    marks[m] = step.mark(ins)

                    dve.wait_ge(s_halo, it)
                    dve.wait_ge(s_hz, seq + 1)
                    taps((4, 5))
                    dve.wait_ge(s_ad, NA * it + AI["dt"] + 1 + ACT_BANKS)
                    per_chunk = lambda ap: ap.unsqueeze(1).broadcast_to([P, CH, HEADS])
                    chunks = lambda ap: ap.rearrange("p (c h) -> p c h", c=CH)
                    nc.vector.tensor_tensor(chunks(v_dt), chunks(dt_raw), per_chunk(dt_bias_b[:]),
                                            ALU.add).then_inc(s_dtv, 1)
                    taps((0, 1))
                    dve.wait_ge(s_dtl, it + 1)
                    step.link(nc.vector.tensor_scalar(c_dt, e_dt, 1.0, -1.0, ALU.add, ALU.add))
                    step.link(nc.vector.tensor_tensor(r_dt, e_dt, c_dt, ALU.subtract))
                    step.link(nc.vector.tensor_tensor(l_dt, ln_dt, r_dt, ALU.add))
                    step.link(nc.vector.scalar_tensor_tensor(out=dt, in0=v_dt, scalar=0.0, in1=l_dt,
                                                             op0=ALU.max, op1=ALU.add))
                    nc.vector.tensor_tensor(chunks(a), chunks(dt), per_chunk(neg_a[:]), ALU.mult).then_inc(s_a, 1)
                    taps((2, 3))
                    dve.wait_ge(s_cv, MC * it + MC)
                    nc.vector.tensor_copy(xp[:, :, 0:HALO], xp[:, :, TILE:]).then_inc(s_halo, 1)

                    def pre(c):
                        b = item(f"gb{c}")
                        if c >= 2:
                            dve.wait_ge(s_M, CH * it + c - 1)
                            dve.wait_ge(s_si, CH * it + c - 1)
                        g = step.mark(nc.vector.tensor_tensor(Gm[:, c % 2, :], b[:, 0:P], tri_le[:], ALU.mult))
                        nc.vector.tensor_copy(Bt[:, c % 2, :], b[:, P:2 * P]).then_inc(s_dd, 1)
                        dve.wait_ge(s_ad, NA * it + AI[f"dhi{c}"] + 1 + ACT_BANKS)
                        step.wait(g)
                        e = E[:, c % 2, :, :]
                        nc.vector.tensor_tensor(e, e, Gm[:, c % 2, :].unsqueeze(1).broadcast_to([P, HEADS, P]),
                                                ALU.mult).then_inc(s_M, 1)

                    def main(c):
                        yc, hs = y[:, c % 2, :], slice(c * HEADS, (c + 1) * HEADS)
                        b = item(f"yoff{c}")
                        dve.wait_ge(s_u, 3 * (CH * it + c) + 3)
                        nc.vector.tensor_tensor(heads(tmp[:]), heads(b[:]),
                                                dec[:, 0, hs].unsqueeze(2).broadcast_to([P, HEADS, HDIM]),
                                                ALU.mult).then_inc(s_dd, 1)
                        b = item(f"ydiag{c}")
                        step.link(nc.vector.tensor_tensor(yc, yc, b[:], ALU.add))
                        nc.vector.tensor_tensor(tmp[:], tmp[:], yc, ALU.add).then_inc(s_dd, 1)
                        dve.wait_ge(s_si, CH * it + c + 1)
                        dve.wait_ge(s_sdec, CH * it + c + 1)
                        o = 1 - c % 2
                        nc.vector.tensor_tensor(S[:, o, :], S[:, o, :], st_bank[:], ALU.add).then_inc(s_sup, 1)
                        dve.wait_ge(s_dd, ND * it + DI[f"ydiag{c}"] + 1 + DVE_BANKS)
                        nc.vector.tensor_tensor(yc, tmp[:], z_s[:, c, :], ALU.mult).then_inc(s_y, 1)

                    def tail(c):
                        lo_part(f"yT{c}", KD + c + 1, yT_hi[:].rearrange("p k n -> p (k n)"),
                                yT_lo[:].rearrange("p k n -> p (k n)"))
                        b = item(f"wo{c}")
                        dve.wait_ge(s_rsy, CH * it + c + 1)
                        dve.wait_ge(s_xres, it + 1)
                        nc.vector.scalar_tensor_tensor(out=h[:, c, :], in0=b[:, 0:D], scalar=rsy[:, c:c + 1],
                                                       in1=x_res[:, c, :], op0=ALU.mult, op1=ALU.add).then_inc(s_dd, 1)

                    pre(0)
                    for c in range(CH):
                        if c < CH - 1:
                            pre(c + 1)
                        main(c)
                        if c > 0:
                            tail(c - 1)
                    tail(CH - 1)
                    for k in range(KD):
                        lo_part(f"hT{k}", KD + CH + k + 1, hT_hi[:, k, :], hT_lo[:, k, :])
                    for j in range(KH):
                        dve.wait_ge(s_mh, KH * it + j + 1)
                        nc.vector.tensor_tensor(m_lo[:, j % 2, :], m_fc[:, j % 2, :], m_hi[:, j % 2, :].bitcast(F32),
                                                ALU.subtract).then_inc(s_ml, 1)
                    dve.wait_ge(s_rsh, it + 1)
                    dve.wait_ge(s_dd, ND * it + ND + DVE_BANKS)
                    xh = [step.mark(nc.vector.tensor_tensor(x_res[:, c, :], x_res[:, c, :], h[:, c, :], ALU.add))
                          for c in range(CH)]
                    dve.wait_ge(s_pj, KH * it + KH)
                    dve.wait_ge(s_x1o, 16 * it)
                    for c in range(CH):
                        step.wait(xh[c])
                        nc.vector.scalar_tensor_tensor(
                            out=x1[:, c, :], in0=pj_banks[c // 2][:, (c % 2) * D:(c % 2 + 1) * D], scalar=r2h[:, c:c + 1],
                            in1=x_res[:, c, :], op0=ALU.mult, op1=ALU.add).then_inc(s_pjd, 1)
                    dve.wait_ge(s_pjd, CH * it + CH)
                    row_stats(nc, step, x1, bn, mv, lambda ins: ins.then_inc(s_mv, 1))
                    dve.wait_ge(s_rsv, it + 1)
                    for c in range(CH):
                        nc.vector.tensor_scalar(x1[:, c, :], x1[:, c, :], mv[:, 0, c:c + 1], rsv[:, c:c + 1],
                                                ALU.subtract, ALU.mult).then_inc(s_x1, 1)
                    assert step.n == D_STEPS, step.n

                D_STEPS = MC * (TAPS - 1) + 4 + CH + CH + CH + STAT_STEPS
                with dve.Fori(0, SEQS) as seq:
                    dve.wait_ge(s_halo, SEQ_TILES * seq)
                    dve.wait_ge(s_cv, MC * SEQ_TILES * seq)
                    nc.vector.memset(xp[:, :, 0:HALO], 0.0).then_inc(s_hz, 1)
                    with dve.Fori(0, SEQ_TILES) as j:
                        tile(seq * SEQ_TILES + j, seq)

        a_ctx.close()

        h1_sb, h2_sb = sb("h1_sb", [P, KH, HID], F32R), sb("h2_sb", [P, KH, HID], F32R)
        w3_sb = sb("w3_sb", [P, KH, D], F32R)
        scale = sb("scale", [P, 4, KH])
        s3_b = sb("s3_b", [P, D])
        x1_in, x1_res = sb("x1_in", [P, CH, D]), sb("x1_res", [P, CH, D])
        x1T_hi, x1T_lo = sb("x1T_hi", [P, KD, TILE], F32R), sb("x1T_lo", [P, KD, TILE], F32R)
        hA_hi, hA_lo = sb("hA_hi", [P, KH, TILE], F32R), sb("hA_lo", [P, KH, TILE], F32R)
        hB_hi, hB_lo = sb("hB_hi", [P, KH, TILE], F32R), sb("hB_lo", [P, KH, TILE], F32R)
        FULL = 3
        full = sb("full", [P, FULL, TILE])
        gate = sb("gate", [P, 2, TILE])
        o_sb = sb("o_sb", [P, CH, D])
        CHK = 2048
        low = sb("low", [P, 2, CHK], I32)
        lowsum = sb("lowsum", [P, 16])
        inexact = sb("inexact", [1, 2])
        bn_b, mv_b = sb("bn_b", [P, CH, 6]), sb("mv_b", [P, 3, CH])
        lnv_b, rsv_b = sb("lnv_b", [P, CH]), sb("rsv_b", [P, CH])

        t_bank = lambda i: banks[B_ACT_BANKS + i % B_DVE_BANKS]
        g_bank = lambda i: banks[i % B_ACT_BANKS]
        acc = banks[6:8]

        s_par = sem("ffn_params_loaded")
        s_h1 = sem("h1_loaded")
        s_h2 = sem("h2_loaded")
        s_w3 = sem("w3_loaded")
        s_low = sem("low_bits_ready")
        s_sum = sem("low_bits_summed")
        s_flagp = sem("inexact_summed")
        s_flag = sem("inexact_ready")
        s_x1i = sem("x1_loaded")
        s_kept = sem("x1_kept")
        s_ti = sem("ffn_dve_item_ready")
        s_td = sem("ffn_dve_item_drained")
        s_gi = sem("ffn_act_item_ready")
        s_gd = sem("ffn_act_item_drained")
        s_thi = sem("x1T_hi_ready")
        s_shi = sem("hidden_hi_ready")
        s_split = sem("hidden_split")
        s_acc = sem("ffn_sum_ready")
        s_accd = sem("ffn_sum_drained")
        s_bstep = sem("ffn_dve_step")
        s_mvb = sem("out_var_ready")
        s_lnb = sem("out_log_var_ready")
        s_rsb = sem("out_rstd_ready")
        s_o = sem("out_ready")
        s_store = sem("out_stored")

        flat = lambda ap: ap[:].rearrange("p k n -> p (k n)")
        pieces = [(flat(w1_sb), 0, None), (flat(w2_sb), 0, None)]
        pieces += [(flat(h1_sb), i * CHK, s_h1) for i in range(KH * HID // CHK)]
        pieces += [(flat(h2_sb), i * CHK, s_h2) for i in range(KH * HID // CHK)]
        pieces += [(flat(w3_sb), 0, s_w3)]
        assert KD * HID == CHK and KH * D == CHK

        with nc.Block() as block:
            @block.sync
            def _(sp):
                def load(at):
                    sp.dma_start(x1_in[:], rows(x1_dram, at)).then_inc(s_x1i, 16)

                def store(it, at):
                    sp.wait_ge(s_o, CH * it + CH)
                    sp.dma_start(rows(out, at), o_sb[:]).then_inc(s_store, 16)

                load(0)
                for i, s in enumerate((s1, s2, sh1, sh2)):
                    sp.dma_start(scale[:, i, :], s).then_inc(s_par, 16)
                sp.dma_start(s3_b[:], s3.partition_broadcast(P)).then_inc(s_par, 16)
                for dst, name, s in ((h1_sb, "h1", s_h1), (h2_sb, "h2", s_h2), (w3_sb, "w3", s_w3)):
                    sp.dma_start(dst[:].bitcast(F32), raw[name].rearrange("(k p) n -> p k n", p=P)).then_inc(s, 16)
                with sp.Fori(0, TILES - 1) as it:
                    at, at_next = sp.snap(it * (TILE * D)), sp.snap((it + 1) * (TILE * D))
                    sp.wait_ge(s_td, NBD * it + KD + B_DVE_BANKS)
                    load(at_next)
                    store(it, at)
                store(TILES - 1, (N - TILE) * D)
                sp.wait_ge(s_store, 16 * TILES)

            @block.tensor
            def _(pe):
                def tile(it, exact):
                    def two(o, w, hi, lo, first, last, rows_out=False):
                        for n, v in enumerate((lo, hi)):
                            ww, vv = (w, v) if exact else (w.bitcast(F32), v.bitcast(F32))
                            a_, b_ = (vv, ww) if rows_out else (ww, vv)
                            ins = pe.matmul(o, a_, b_, start=first and n == 0, stop=last and n == 1,
                                            skip_group_check=True)
                        return ins

                    def g_item(i):
                        pe.wait_ge(s_gd, NBA * it + i + 1)
                        return g_bank(i)

                    def t_item(i):
                        pe.wait_ge(s_td, NBD * it + i + 1)
                        return t_bank(i)

                    pe.wait_ge(s_x1i, 16 * it + 16)
                    for k in range(KD):
                        b = t_item(k)
                        for c in range(CH):
                            last = pe.transpose(b[:, c * P:(c + 1) * P], x1_in[:, c, k * P:(k + 1) * P], ident[:])
                        last.then_inc(s_ti, 1)
                    pe.wait_ge(s_td, NBD * it + KD + B_DVE_BANKS)
                    for j in range(KH):
                        cols = slice(j * P, (j + 1) * P)
                        for w, b, s in ((w1_sb, g_item(j), s_gi), (w2_sb, t_item(KD + j), s_ti)):
                            for k in range(KD):
                                last = two(b[:], w[:, k, cols], x1T_hi[:, k, :], x1T_lo[:, k, :], k == 0, k == KD - 1)
                            last.then_inc(s, 1)

                    def hidden(layer, w, hi, lo, after=None):
                        for j in range(KH):
                            b = g_item(layer * KH + j)
                            cols = slice(j * P, (j + 1) * P)
                            for k in range(KH):
                                if j == 0:
                                    pe.wait_ge(s_split, 3 * KH * it + (layer - 1) * KH + k + 1)
                                last = two(b[:], w[:, k, cols], hi[:, k, :], lo[:, k, :], k == 0, k == KH - 1)
                            last.then_inc(s_gi, 1)
                            if after and j > 0:
                                after(j - 1)

                    def out_rows(j):
                        pe.wait_ge(s_split, 3 * KH * it + 2 * KH + j + 1)
                        if j == 0:
                            pe.wait_ge(s_accd, 2 * it)
                        for c in range(CH):
                            tok = slice(c * P, (c + 1) * P)
                            last = two(acc[c // 2][:, (c % 2) * D:(c % 2 + 1) * D], w3_sb[:, j, :], hA_hi[:, j, tok],
                                       hA_lo[:, j, tok], j == 0 and c % 2 == 0, j == KH - 1, rows_out=True)
                        last.then_inc(s_acc, 1)

                    hidden(1, h1_sb, hA_hi, hA_lo)
                    hidden(2, h2_sb, hB_hi, hB_lo, out_rows)
                    out_rows(KH - 1)

                pe.wait_ge(s_sum, len(pieces) + 1)
                pe.matmul(banks[0][0:1, 0:2], lowsum[:, 12:13], ones[:, 0:2], start=True, stop=True).then_inc(s_flagp, 1)
                pe.wait_ge(s_flag, 1)
                bits = pe.value_load(inexact[0:1, 0:1].bitcast(I32))
                with pe.If(bits == 0):
                    with pe.Fori(0, TILES) as it:
                        tile(it, True)
                with pe.Else():
                    with pe.Fori(0, TILES) as it:
                        tile(it, False)

            @block.scalar
            def _(act):
                act.sem_inc(s_gd, B_ACT_BANKS)
                for i in range(len(pieces)):
                    act.wait_ge(s_low, i + 1)
                    act.wait_ge(s_sum, i)
                    nc.scalar.activation(low[:, i % 2, :].bitcast(F32), low[:, i % 2, :], ACT.Copy,
                                         accum_out=lowsum[:, i:i + 1]).then_inc(s_sum, 1)
                act.wait_ge(s_par, 80)
                with act.Fori(0, TILES) as it:
                    def item(i):
                        act.wait_ge(s_gi, NBA * it + i + 1)
                        return g_bank(i)

                    for k in range(KD):
                        act.wait_ge(s_ti, NBD * it + k + 1)
                        nc.scalar.activation(x1T_hi[:, k, :], t_bank(k)[:], ACT.Copy).then_inc(s_thi, 1)
                    for j in range(KH):
                        b = item(j)
                        if j >= 2:
                            act.wait_ge(s_td, NBD * it + KD + j - 1 + B_DVE_BANKS)
                        nc.scalar.activation(gate[:, j % 2, :], b[:], ACT.Silu, scale=scale[:, 0, j:j + 1]).then_inc(s_gd, 1)
                    for n in range(KH, 3 * KH):
                        b = item(n)
                        act.wait_ge(s_split, 3 * KH * it + n - FULL + 1)
                        nc.scalar.activation(full[:, n % FULL, :], b[:], ACT.Gelu,
                                             scale=scale[:, 1 + n // KH, n % KH:n % KH + 1]).then_inc(s_gd, 1)
                    act.wait_ge(s_mvb, it + 1)
                    nc.scalar.activation(lnv_b[:], mv_b[:, 1, :], ACT.Ln, scale=1.0 / D, bias=eps[:, 2:3]).then_inc(s_lnb, 1)
                    act.wait_ge(s_lnb, it + 1)
                    nc.scalar.activation(rsv_b[:], lnv_b[:], ACT.Exp, scale=-0.5).then_inc(s_rsb, 1)

            @block.vector
            def _(dve):
                dve.sem_inc(s_td, B_DVE_BANKS)
                for i, (w, at, s) in enumerate(pieces):
                    if s is not None:
                        dve.wait_ge(s, 16)
                    if i >= 2:
                        dve.wait_ge(s_sum, i - 1)
                    nc.vector.tensor_scalar(low[:, i % 2, :], w[:, at:at + CHK].bitcast(I32), LOW_BITS, None,
                                            ALU.bitwise_and).then_inc(s_low, 1)
                dve.wait_ge(s_sum, len(pieces))
                nc.vector.reduce_sum(lowsum[:, 12:13], lowsum[:, 0:len(pieces)], AX.X).then_inc(s_sum, 1)
                dve.wait_ge(s_flagp, 1)
                nc.vector.tensor_copy(inexact[:], banks[0][0:1, 0:2]).then_inc(s_flag, 1)
                dve.wait_ge(s_par, 80)
                B_STEPS = 2 + STAT_STEPS
                with dve.Fori(0, TILES) as it:
                    step = Steps(dve, s_bstep, B_STEPS * it)
                    dve.wait_ge(s_x1i, 16 * it + 16)
                    dve.wait_ge(s_kept, it)
                    nc.vector.tensor_copy(x1_res[:], x1_in[:]).then_inc(s_kept, 1)
                    for k in range(KD):
                        dve.wait_ge(s_thi, KD * it + k + 1)
                        nc.vector.tensor_tensor(x1T_lo[:, k, :], t_bank(k)[:], x1T_hi[:, k, :].bitcast(F32),
                                                ALU.subtract).then_inc(s_td, 1)

                    def split(n, hi, lo):
                        nc.vector.tensor_copy(hi, full[:, n % FULL, :]).then_inc(s_shi, 1)
                        dve.wait_ge(s_shi, 3 * KH * it + n + 1)
                        nc.vector.tensor_tensor(lo, full[:, n % FULL, :], hi.bitcast(F32), ALU.subtract).then_inc(s_split, 1)

                    def gated(j):
                        dve.wait_ge(s_ti, NBD * it + KD + j + 1)
                        dve.wait_ge(s_gd, NBA * it + j + 1 + B_ACT_BANKS)
                        nc.vector.scalar_tensor_tensor(out=full[:, j % FULL, :], in0=t_bank(KD + j)[:],
                                                       scalar=scale[:, 1, j:j + 1], in1=gate[:, j % 2, :],
                                                       op0=ALU.mult, op1=ALU.mult).then_inc(s_td, 1)

                    for j in range(KH):
                        gated(j)
                        dve.wait_ge(s_td, NBD * it + KD + j + 1 + B_DVE_BANKS)
                        split(j, hA_hi[:, j, :], hA_lo[:, j, :])
                    for n in range(KH, 3 * KH):
                        dve.wait_ge(s_gd, NBA * it + n + 1 + B_ACT_BANKS)
                        hi, lo = (hB_hi, hB_lo) if n < 2 * KH else (hA_hi, hA_lo)
                        split(n, hi[:, n % KH, :], lo[:, n % KH, :])
                    dve.wait_ge(s_acc, KH * it + KH)
                    dve.wait_ge(s_store, 16 * it)
                    for i in range(2):
                        o = o_sb[:, 2 * i:2 * i + 2, :]
                        nc.vector.tensor_tensor(o, acc[i][:].rearrange("p (c n) -> p c n", c=2),
                                                s3_b[:].unsqueeze(1).broadcast_to([P, 2, D]), ALU.mult).then_inc(s_accd, 1)
                    for i in range(2):
                        o = o_sb[:, 2 * i:2 * i + 2, :]
                        dve.wait_ge(s_accd, 2 * it + i + 1)
                        step.mark(nc.vector.tensor_tensor(o, o, x1_res[:, 2 * i:2 * i + 2, :], ALU.add))
                    step.wait(step.n)
                    row_stats(nc, step, o_sb, bn_b, mv_b, lambda ins: ins.then_inc(s_mvb, 1))
                    assert step.n == B_STEPS
                    dve.wait_ge(s_rsb, it + 1)
                    for c in range(CH):
                        nc.vector.tensor_scalar(o_sb[:, c, :], o_sb[:, c, :], mv_b[:, 0, c:c + 1], rsv_b[:, c:c + 1],
                                                ALU.subtract, ALU.mult).then_inc(s_o, 1)


def kernel(**inputs):
    import numpy as np
    import concourse.bacc as bacc
    from concourse.bass_utils import run_bass_kernel_spmd as run

    get = lambda name: np.asarray(inputs[name])
    channels = lambda v: np.ascontiguousarray(v.reshape(-1, P).T)
    x = get("L0_attn_x")
    batch, seq, width = x.shape
    f, g = "L0_attn_", "L0_ffn_"
    arrays = {
        "x": x.reshape(-1, width),
        "w_in": get(f + "w_in"),
        "conv_w": np.ascontiguousarray(get(f + "conv_w").reshape(-1, P, TAPS).transpose(1, 0, 2)),
        "conv_b": channels(get(f + "conv_b")),
        "dt_bias": get(f + "dt_bias"),
        "a_log": get(f + "a_log"),
        "d_skip": get(f + "d_skip"),
        "norm_w": channels(get(f + "norm_w")),
        "w_out": get(f + "w_out"),
        "w_fc": get(f + "w_fc"),
        "w_proj": get(f + "w_proj"),
        "w1": get(g + "w1_w").T, "s1": channels(get(g + "w1_s")),
        "w2": get(g + "w2_w").T, "s2": channels(get(g + "w2_s")),
        "h1": get(g + "h1_w").T, "sh1": channels(get(g + "h1_s")),
        "h2": get(g + "h2_w").T, "sh2": channels(get(g + "h2_s")),
        "w3": get(g + "w3_w").T, "s3": get(g + "w3_s"),
    }
    arrays = {n: np.ascontiguousarray(a) for n, a in arrays.items()}
    nc = bacc.Bacc("TRN2", target_bir_lowering=False, num_devices=1)
    args = [nc.dram_tensor(n, a.shape, mybir.dt.from_np(a.dtype), kind="ExternalInput").ap()
            for n, a in arrays.items()]
    out = nc.dram_tensor("out", arrays["x"].shape, F32, kind="ExternalOutput").ap()
    post_ln_block(nc, *args, out, seq)
    r = run(nc, [arrays], core_ids=[0])
    return r.results[0]["out"].reshape(batch, seq, width)
```

```python
from contextlib import ExitStack

import concourse.bass as bass
from concourse import mybir

F32 = mybir.dt.float32
F32R = mybir.dt.float32r
I32 = mybir.dt.int32
ALU = mybir.AluOpType
ACT = mybir.ActivationFunctionType
AX = mybir.AxisListType

P = 128
TILE = 512
CH = TILE // P
D = 256
KD = D // P
INNER = 512
KI = INNER // P
HEADS = 8
HDIM = INNER // HEADS
CONV = INNER + 2 * P
MC = CONV // P
TAPS = 4
HALO = TAPS - 1
PROJ = 2 * INNER + 2 * P + HEADS
HID = 4 * D
KH = HID // P
EPS_OUT = 1.1920929e-07
EPS_GATE = 1e-05
EPS_LN = 1e-05
LOW_BITS = 0xFFF

CONV_ORDER = (4, 5, 0, 1, 2, 3)
F_ACT = ["dt"] + [f"xbc{m}" for m in CONV_ORDER] + [f"z{c}" for c in range(CH)]
C_ACT = ["cums"] + [f"{n}{c}" for c in range(CH) for n in ("xt", "dlo", "dhi")]
M_ACT = [f"fc{j}" for j in range(KH)]
FM_ACT = F_ACT[:7] + [n for c in range(CH) for n in (f"fc{c}", f"z{c}")] + M_ACT[CH:]
C_DVE = ["gb0"]
for _c in range(CH):
    C_DVE += [f"gb{_c + 1}"] * (_c < CH - 1) + [f"yT{_c - 1}"] * (_c > 0)
    C_DVE += [f"yoff{_c}", f"ydiag{_c}"] + [f"wo{_c - 1}"] * (_c > 0)
F_DVE = ["xnT0", "xnT1"]
TURN_XN = CH - 2
_at = C_DVE.index(f"wo{TURN_XN - 1}") + 1
CF_DVE = C_DVE[:_at] + F_DVE + C_DVE[_at:]
M_DVE = [f"yT{CH - 1}", f"wo{CH - 1}", "hT0", "hT1"]
FIRST = (F_ACT, F_DVE, F_DVE)
HI = lambda order: [n for n in order if "T" in n]
LOOP = (C_ACT + FM_ACT, CF_DVE + M_DVE, HI(CF_DVE + M_DVE))
LAST = (C_ACT + M_ACT, C_DVE + M_DVE, HI(C_DVE + M_DVE))
ACT_BANKS, DVE_BANKS = 2, 3
assert len(LOOP[0]) % ACT_BANKS == 0 and len(LOOP[1]) % DVE_BANKS == 0

B_ACT_BANKS, B_DVE_BANKS = 4, 2
NBA, NBD = 3 * KH, KD + KH
FFN_COLS = {"w1": (0, KD, HID), "w2": (KD * HID, KD, HID), "h1": (2 * KD * HID, KH, HID),
            "h2": ((2 * KD + KH) * HID, KH, HID), "w3": ((2 * KD + 2 * KH) * HID, KH, D)}
FFN_WORDS = (2 * KD + 2 * KH) * HID + KH * D
CHECKS = 4


class Where:

    def __init__(self, orders, i):
        self.orders = orders
        self.base = [0 if orders is FIRST else len(f) + len(o) * i for f, o in zip(FIRST, LOOP)]
        self.first = [0 if orders is FIRST else len(f) for f in FIRST]

    def act(self, name):
        return self.base[0] + self.orders[0].index(name)

    def dve(self, name):
        return self.base[1] + self.orders[1].index(name)

    def hi(self, name):
        return self.base[2] + self.orders[2].index(name)

    def act_bank(self, name):
        return (self.first[0] + self.orders[0].index(name)) % ACT_BANKS

    def dve_bank(self, name):
        return ACT_BANKS + (self.first[1] + self.orders[1].index(name)) % DVE_BANKS


def ge(eng, s, value):
    if not (isinstance(value, int) and value <= 0):
        eng.wait_ge(s, value)


def post_ln_block(nc, x, w_in, conv_w, conv_b, dt_bias, a_log, d_skip, norm_w, w_out, w_fc, w_proj,
                  w_ffn, s1, s2, sh1, sh2, s3, out, seq_len):
    N = x.shape[0]
    TILES = N // TILE
    SEQ_TILES = seq_len // TILE
    PIECE = FFN_WORDS // TILES
    LOW = PIECE // CHECKS
    assert PIECE * TILES == FFN_WORDS and LOW * CHECKS == PIECE and KH * D <= PIECE

    ctx = ExitStack()
    with ctx:
        def sb(name, shape, dt=F32, into=ctx):
            return into.enter_context(nc.sbuf_tensor(name, shape, dt))

        def sem(name):
            return ctx.enter_context(nc.semaphore(name))

        class Steps:

            def __init__(self, eng, s, base):
                self.eng, self.s, self.base, self.n = eng, s, base, 0

            def mark(self, ins):
                self.n += 1
                ins.then_inc(self.s, 1)
                return self.n

            def wait(self, n):
                self.eng.wait_ge(self.s, self.base + n)

            def link(self, ins):
                self.wait(self.mark(ins))

        def layer_norm_stats(step, src, bn, mv, eps):
            for c in range(CH):
                step.mark(nc.vector.bn_stats(bn[:, c, :], src[:, c, :]))
            step.wait(step.n)
            tt, ts = nc.vector.tensor_tensor, nc.vector.tensor_scalar
            step.mark(tt(mv[:, 0, :], bn[:, :, 1], bn[:, :, 4], ALU.add))
            step.mark(tt(mv[:, 2, :], bn[:, :, 1], bn[:, :, 4], ALU.subtract))
            step.link(tt(mv[:, 1, :], bn[:, :, 2], bn[:, :, 5], ALU.add))
            step.mark(ts(mv[:, 0, :], mv[:, 0, :], 0.5, None, ALU.mult))
            step.mark(tt(mv[:, 2, :], mv[:, 2, :], mv[:, 2, :], ALU.mult))
            step.link(ts(mv[:, 1, :], mv[:, 1, :], 1.0 / D, eps, ALU.mult, ALU.add))
            return nc.vector.scalar_tensor_tensor(out=mv[:, 1, :], in0=mv[:, 2, :], scalar=0.25,
                                                  in1=mv[:, 1, :], op0=ALU.mult, op1=ALU.add)

        STAT_STEPS = CH + 6
        rows = lambda ap, at: (ap.rearrange("n f -> (n f)")[bass.ds(at, TILE * D)]
                               .rearrange("(c p f) -> p c f", p=P, f=D))

        banks = [ctx.enter_context(nc.psum_tensor(f"bank{i}", [P, 512], F32)) for i in range(8)]

        raw = nc.dram_tensor("ffn_raw", (P, FFN_WORDS), F32, kind="Internal").ap()
        x1_dram = nc.dram_tensor("x1_rows", (N, D), F32, kind="Internal").ap()

        ident, ones = sb("ident", [P, P]), sb("ones", [P, P])
        eps = sb("eps", [P, 4])
        lowsum = sb("lowsum", [P, TILES * CHECKS])

        s_params = sem("params_loaded")
        s_masks = sem("masks_ready")
        s_stage = [sem(f"{n}_staged") for n in ("w_in", "w_out", "w_fc", "w_proj")]
        s_nw = sem("w_out_scaled")
        s_whi = sem("weight_hi_ready")
        s_wlo = sem("weight_lo_ready")
        s_nega = sem("neg_a_ready")

        a_ctx = ctx.enter_context(ExitStack())
        A = lambda name, shape, dt=F32: sb(name, shape, dt, a_ctx)
        tri_le = A("tri_le", [P, P])
        tri_gt = A("tri_gt", [P, P])
        keep = A("keep", [P, TILES], I32)
        w_in_hi, w_in_lo = A("w_in_hi", [P, KD, PROJ], F32R), A("w_in_lo", [P, KD, PROJ], F32R)
        w_out_hi, w_out_lo = A("w_out_hi", [P, KI, D], F32R), A("w_out_lo", [P, KI, D], F32R)
        w_fc_hi, w_fc_lo = A("w_fc_hi", [P, KD, HID], F32R), A("w_fc_lo", [P, KD, HID], F32R)
        w_pj_hi, w_pj_lo = A("w_pj_hi", [P, KH, D], F32R), A("w_pj_lo", [P, KH, D], F32R)
        conv_w_sb, conv_b_sb = A("conv_w_sb", [P, MC, TAPS]), A("conv_b_sb", [P, MC])
        dt_bias_b, neg_a, dskip_b = A("dt_bias_b", [P, HEADS]), A("neg_a", [P, HEADS]), A("dskip_b", [P, HEADS])
        norm_w_sb, a_log_b = A("norm_w_sb", [P, KI]), A("a_log_b", [P, HEADS])

        x_in, x_res = A("x_in", [P, CH, D]), A("x_res", [P, CH, D])
        junk = A("junk", [P, INNER])
        xn = A("xn", [P, CH, D])
        xnT_hi, xnT_lo = A("xnT_hi", [P, KD, TILE], F32R), A("xnT_lo", [P, KD, TILE], F32R)
        xp = A("xp", [P, MC, HALO + TILE])
        xc = A("xc", [P, MC, TILE])
        z_s = A("z_s", [P, CH, INNER])
        dtT = A("dtT", [P, TILE])
        sm = A("sm", [P, 9, CH * HEADS])
        v_dt, ab_dt, e_dt, ln_dt, c_dt, r_dt, l_dt, dt, a = (sm[:, i, :] for i in range(9))
        dec = A("dec", [P, 3, CH * HEADS])
        stat = A("stat", [P, 9, CH])
        ssx, lnx, rsx, ssy, lny, rsy, ssh, lnh, r2h = (stat[:, i, :] for i in range(9))
        bn, mv, rsv = A("bn", [P, CH, 6]), A("mv", [P, 3, CH]), A("rsv", [P, CH])
        RA = A("RA", [P, 2, HEADS, P])
        E = A("E", [P, 2, HEADS, P])
        Gm, Bt = A("Gm", [P, 2, P]), A("Bt", [P, 2, P])
        xt, u, ud, y = (A(n, [P, 2, INNER]) for n in ("xt", "u", "ud", "y"))
        S = A("S", [P, 2, INNER])
        tmp = A("tmp", [P, INNER])
        yT_hi, yT_lo = A("yT_hi", [P, KI, P], F32R), A("yT_lo", [P, KI, P], F32R)
        h = A("h", [P, CH, D])
        hT_hi, hT_lo = A("hT_hi", [P, KD, TILE], F32R), A("hT_lo", [P, KD, TILE], F32R)
        m_fc = A("m_fc", [P, 2, TILE])
        m_hi, m_lo = A("m_hi", [P, 2, TILE], F32R), A("m_lo", [P, 2, TILE], F32R)
        x1 = A("x1", [P, CH, D])
        chk = A("chk", [P, PIECE])
        low = A("low", [P, LOW], I32)

        st_bank = banks[5]
        pj_banks = banks[6:8]
        staged = [(xp[:].rearrange("p m n -> p (m n)")[:, 0:KD * PROJ], w_in_hi, w_in_lo, w_in),
                  (x1[:].rearrange("p c n -> p (c n)"), w_out_hi, w_out_lo, w_out),
                  (E[:].rearrange("p b h n -> p (b h n)"), w_fc_hi, w_fc_lo, w_fc),
                  (chk[:, 0:KH * D], w_pj_hi, w_pj_lo, w_proj)]
        flat3 = lambda ap: ap[:].rearrange("p k n -> p (k n)")

        s_x = sem("x_loaded")
        s_xres = sem("x_kept")
        s_rsx = sem("x_rstd_ready")
        s_xn = sem("xn_ready")
        s_ai = sem("act_item_ready")
        s_ad = sem("act_item_drained")
        s_di = sem("dve_item_ready")
        s_dd = sem("dve_item_drained")
        s_hi = sem("activation_hi_ready")
        s_dtl = sem("dt_log_ready")
        s_dtv = sem("dt_biased")
        s_a = sem("a_ready")
        s_cv = sem("conv_ready")
        s_xc = sem("xc_ready")
        s_halo = sem("halo_kept")
        s_start = sem("halo_and_state_cleared")
        s_ra = sem("masked_a_ready")
        s_M = sem("decayed_scores_ready")
        s_u = sem("u_ready")
        s_sdec = sem("state_decayed")
        s_si = sem("state_item_ready")
        s_sup = sem("state_updated")
        s_y = sem("y_ready")
        s_rsy = sem("y_rstd_ready")
        s_r2h = sem("h_rstd_ready")
        s_m = sem("m_ready")
        s_mh = sem("m_hi_ready")
        s_ml = sem("m_lo_ready")
        s_mld = sem("m_lo_ready_by_dve")
        s_dtt = sem("dt_turned")
        s_pj = sem("proj_ready")
        s_pjd = sem("proj_drained")
        s_mv = sem("ln_var_ready")
        s_rsv = sem("ln_rstd_ready")
        s_x1 = sem("x1_ready")
        s_x1o = sem("x1_stored")
        s_chk = sem("ffn_piece_loaded")
        s_raw = sem("ffn_piece_stored")
        s_low = sem("low_bits_ready")
        s_sum = sem("low_bits_summed")
        s_as = sem("act_step")
        s_ds = sem("dve_step")

        def m_split(eng, i, j):
            if j < CH:
                eng.wait_ge(s_ml, CH * i + j + 1)
            else:
                eng.wait_ge(s_mld, (KH - CH) * i + j - CH + 1)

        MASKS = 12

        with nc.Block() as block:
            @block.sync
            def _(sp):
                def load_x(t, at):
                    ge(sp, s_xres, t)
                    sp.dma_start(x_in[:], rows(x, at)).then_inc(s_x, 16)

                def load_piece(i, at, stored):
                    ge(sp, s_low, CHECKS * i)
                    ge(sp, s_raw, stored)
                    sp.dma_start(chk[:], w_ffn[:, bass.ds(at, PIECE)]).then_inc(s_chk, 16)

                def store_piece(i, at):
                    sp.wait_ge(s_chk, 16 * i + 16)
                    sp.dma_start(raw[:, bass.ds(at, PIECE)], chk[:]).then_inc(s_raw, 16)

                def store_x1(i, at):
                    sp.wait_ge(s_x1, CH * i + CH)
                    sp.dma_start(rows(x1_dram, at), x1[:]).then_inc(s_x1o, 16)

                sp.sem_inc(s_x1o, 1)
                load_x(0, 0)
                for (dst, hi, lo, src), s in zip(staged, s_stage):
                    sp.dma_start(dst.rearrange("p (k n) -> p k n", n=src.shape[1]),
                                 src.rearrange("(k p) n -> p k n", p=P)).then_inc(s, 16)
                    if s is s_stage[0]:
                        for dst, src in ((a_log_b, a_log.partition_broadcast(P)),
                                         (dt_bias_b, dt_bias.partition_broadcast(P)),
                                         (dskip_b, d_skip.partition_broadcast(P)),
                                         (norm_w_sb, norm_w), (conv_w_sb, conv_w), (conv_b_sb, conv_b)):
                            sp.dma_start(dst[:], src).then_inc(s_params, 16)
                sp.wait_ge(s_wlo, len(staged))
                load_piece(0, 0, 0)
                with sp.Fori(0, TILES - 1) as i:
                    at, at_next = sp.snap(i * (TILE * D)), sp.snap((i + 1) * (TILE * D))
                    p_at, p_next = sp.snap(i * PIECE), sp.snap((i + 1) * PIECE)
                    stored = sp.snap(16 * i + 16)
                    load_x(i + 1, at_next)
                    store_piece(i, p_at)
                    store_x1(i, at)
                    load_piece(i + 1, p_next, stored)
                store_piece(TILES - 1, (TILES - 1) * PIECE)
                store_x1(TILES - 1, (TILES - 1) * TILE * D)
                sp.wait_ge(s_x1o, 16 * TILES + 1)
                sp.wait_ge(s_raw, 16 * TILES)

            @block.tensor
            def _(pe):
                def three(o, hi, lo, rhi, rlo, first, last):
                    pe.matmul(o, lo, rhi, start=first, stop=False, skip_group_check=True)
                    pe.matmul(o, hi, rlo, start=False, stop=False, skip_group_check=True)
                    return pe.matmul(o, hi, rhi, start=False, stop=last, skip_group_check=True)

                def act_item(w, name):
                    pe.wait_ge(s_ad, w.act(name) + 1)
                    return banks[w.act_bank(name)]

                def dve_item(w, name):
                    pe.wait_ge(s_dd, w.dve(name) + 1)
                    return banks[w.dve_bank(name)]

                def dve_drained(w, name):
                    pe.wait_ge(s_dd, w.dve(name) + 1 + DVE_BANKS)

                def turn_xn(w, t):
                    pe.wait_ge(s_xn, CH * t + CH)
                    for k in range(KD):
                        b = dve_item(w, f"xnT{k}")
                        for c in range(CH):
                            last = pe.transpose(b[:, c * P:(c + 1) * P], xn[:, c, k * P:(k + 1) * P], ident[:])
                        last.then_inc(s_di, 1)

                def xbc(w, m):
                    b = act_item(w, f"xbc{m}")
                    cols = slice(INNER + m * P, INNER + (m + 1) * P)
                    for k in range(KD):
                        last = three(b[:], w_in_hi[:, k, cols], w_in_lo[:, k, cols],
                                     xnT_hi[:, k, :], xnT_lo[:, k, :], k == 0, k == KD - 1)
                    last.then_inc(s_ai, 1)

                def dt_rows(w):
                    b = act_item(w, "dt")
                    dve_drained(w, "xnT1")
                    cols = slice(PROJ - HEADS, PROJ)
                    for k in range(KD):
                        last = three(b[0:HEADS, :], w_in_hi[:, k, cols], w_in_lo[:, k, cols],
                                     xnT_hi[:, k, :], xnT_lo[:, k, :], k == 0, k == KD - 1)
                    last.then_inc(s_ai, 1)

                def turn_dt(w, t):
                    pe.wait_ge(s_ad, w.act("dt") + 1 + ACT_BANKS)
                    pe.wait_ge(s_sup, CH * t + 1)
                    for c in range(CH):
                        last = pe.transpose(st_bank[:, c * P:(c + 1) * P], dtT[:, c * P:(c + 1) * P], ident[:])
                    last.then_inc(s_dtt, 1)

                def z_rows(w, c):
                    b = act_item(w, f"z{c}")
                    tok = slice(c * P, (c + 1) * P)
                    for k in range(KD):
                        last = three(b[:], xnT_hi[:, k, tok], xnT_lo[:, k, tok],
                                     w_in_hi[:, k, 0:INNER], w_in_lo[:, k, 0:INNER], k == 0, k == KD - 1)
                    last.then_inc(s_ai, 1)

                def sums_of_a(w, i):
                    b = act_item(w, "cums")
                    pe.wait_ge(s_a, i + 1)
                    for n, tri in enumerate((tri_le, tri_gt, ones)):
                        last = pe.matmul(b[:, n * CH * HEADS:(n + 1) * CH * HEADS], tri[:], a, start=True, stop=True)
                    last.then_inc(s_ai, 1)

                def pre(w, i, c):
                    tok = slice(c * P, (c + 1) * P)
                    b = act_item(w, f"xt{c}")
                    pe.wait_ge(s_xc, MC * i + MC)
                    for m in range(KI):
                        last = pe.transpose(b[:, m * P:(m + 1) * P], xc[:, m, tok], ident[:])
                    last.then_inc(s_ai, 1)
                    b = dve_item(w, f"gb{c}")
                    pe.transpose(b[:, P:2 * P], xc[:, KI, tok], ident[:])
                    pe.matmul(b[:, 0:P], xc[:, KI, tok], xc[:, KI + 1, tok], start=True, stop=True,
                              skip_group_check=True).then_inc(s_di, 1)
                    for half, name in enumerate(("dlo", "dhi")):
                        b = act_item(w, f"{name}{c}")
                        pe.wait_ge(s_ra, CH * i + c + 1)
                        src = RA[:, c % 2, half * 4:half * 4 + 4, :].rearrange("p h l -> p (h l)")
                        pe.matmul(b[:], tri_gt[:], src, start=True, stop=True).then_inc(s_ai, 1)

                def main(w, i, c):
                    tok = slice(c * P, (c + 1) * P)
                    b = dve_item(w, f"yoff{c}")
                    pe.wait_ge(s_sdec, CH * i + c + 1)
                    pe.matmul(b[:], xc[:, KI + 1, tok], S[:, c % 2, :], start=True, stop=True).then_inc(s_di, 1)
                    b = dve_item(w, f"ydiag{c}")
                    pe.wait_ge(s_M, CH * i + c + 1)
                    pe.wait_ge(s_u, 3 * (CH * i + c) + 2)
                    for n in range(HEADS):
                        hs = slice(n * HDIM, (n + 1) * HDIM)
                        last = pe.matmul(b[:, hs], E[:, c % 2, n, :], u[:, c % 2, hs], start=True, stop=True)
                    last.then_inc(s_di, 1)
                    pe.wait_ge(s_sup, CH * i + c + 1)
                    pe.matmul(st_bank[:], Bt[:, c % 2, :], ud[:, c % 2, :], start=True, stop=True).then_inc(s_si, 1)

                def turn_y(w, i, c):
                    b = dve_item(w, f"yT{c}")
                    pe.wait_ge(s_y, CH * i + c + 1)
                    for k in range(KI):
                        last = pe.transpose(b[:, k * P:(k + 1) * P], y[:, c % 2, k * P:(k + 1) * P], ident[:])
                    last.then_inc(s_di, 1)

                def out_rows(w, i, c):
                    b = dve_item(w, f"wo{c}")
                    dve_drained(w, f"yT{c}")
                    for k in range(KI):
                        last = three(b[:, 0:D], yT_hi[:, k, :], yT_lo[:, k, :],
                                     w_out_hi[:, k, :], w_out_lo[:, k, :], k == 0, k == KI - 1)
                    last.then_inc(s_di, 1)

                def turn_h(w, i):
                    for k in range(KD):
                        b = dve_item(w, f"hT{k}")
                        dve_drained(w, f"wo{CH - 1}")
                        for c in range(CH):
                            last = pe.transpose(b[:, c * P:(c + 1) * P], h[:, c, k * P:(k + 1) * P], ident[:])
                        last.then_inc(s_di, 1)

                def fc(w, i, j):
                    b = act_item(w, f"fc{j}")
                    if j == 0:
                        dve_drained(w, "hT1")
                    cols = slice(j * P, (j + 1) * P)
                    for k in range(KD):
                        last = three(b[:], w_fc_hi[:, k, cols], w_fc_lo[:, k, cols],
                                     hT_hi[:, k, :], hT_lo[:, k, :], k == 0, k == KD - 1)
                    last.then_inc(s_ai, 1)

                def proj(w, i, j):
                    m_split(pe, i, j)
                    if j == 0:
                        pe.wait_ge(s_pjd, CH * i + 1)
                    for c in range(CH):
                        tok = slice(c * P, (c + 1) * P)
                        o = pj_banks[c // 2][:, (c % 2) * D:(c % 2 + 1) * D]
                        last = three(o, m_hi[:, j % 2, tok], m_lo[:, j % 2, tok], w_pj_hi[:, j, :],
                                     w_pj_lo[:, j, :], j == 0 and c % 2 == 0, j == KH - 1)
                    last.then_inc(s_pj, 1)

                def iteration(w, i, more):
                    sums_of_a(w, i)
                    pre(w, i, 0)
                    for c in range(CH):
                        if c < CH - 1:
                            pre(w, i, c + 1)
                        if c > 0:
                            turn_y(w, i, c - 1)
                        main(w, i, c)
                        if c > 0:
                            out_rows(w, i, c - 1)
                        if more and c == TURN_XN:
                            turn_xn(w, i + 1)
                    if more:
                        dt_rows(w)
                        xbc(w, 4)
                    turn_y(w, i, CH - 1)
                    if more:
                        turn_dt(w, i + 1)
                        xbc(w, 5)
                    out_rows(w, i, CH - 1)
                    if more:
                        xbc(w, 0)
                    if more:
                        xbc(w, 1)
                    turn_h(w, i)
                    if more:
                        xbc(w, 2)
                        xbc(w, 3)
                    for j in range(KH):
                        fc(w, i, j)
                        if j > 0:
                            proj(w, i, j - 1)
                        if more and j < CH:
                            z_rows(w, j)
                    proj(w, i, KH - 1)

                w = Where(FIRST, 0)
                pe.wait_ge(s_masks, MASKS)
                turn_xn(w, 0)
                pe.wait_ge(s_wlo, 1)
                dt_rows(w)
                for m in CONV_ORDER:
                    xbc(w, m)
                    if m == CONV_ORDER[0]:
                        turn_dt(w, 0)
                for c in range(CH):
                    z_rows(w, c)
                pe.wait_ge(s_wlo, len(staged))
                with pe.Fori(0, TILES - 1) as i:
                    iteration(Where(LOOP, i), i, True)
                iteration(Where(LAST, TILES - 1), TILES - 1, False)

            @block.scalar
            def _(act):
                LOG_EXP = "natural_log_exp_and_others"
                act.sem_inc(s_ad, ACT_BANKS)
                X_STEPS, DT_STEPS = CH + 1, 2
                C_STEPS = 2 * CH + CH + 1

                def item(w, name):
                    act.wait_ge(s_ai, w.act(name) + 1)
                    return banks[w.act_bank(name)]

                def hi_part(w, name, dst):
                    act.wait_ge(s_di, w.dve(name) + 1)
                    nc.scalar.activation(dst, banks[w.dve_bank(name)][:], ACT.Copy).then_inc(s_hi, 1)

                def x_rms(step, t):
                    act.wait_ge(s_x, 16 * t + 16)
                    for c in range(CH):
                        step.link(nc.scalar.activation(junk[:, 0:D], x_in[:, c, :], ACT.Square,
                                                       accum_out=ssx[:, c:c + 1]))
                    step.link(nc.scalar.activation(lnx, ssx, ACT.Ln, scale=1.0 / D, bias=eps[:, 0:1]))
                    nc.scalar.activation(rsx, lnx, ACT.Exp, scale=-0.5).then_inc(s_rsx, 1)

                def xnT(w):
                    for k in range(KD):
                        hi_part(w, f"xnT{k}", xnT_hi[:, k, :])

                def xbc(w, t, m):
                    b = item(w, f"xbc{m}")
                    if m == CONV_ORDER[0]:
                        ge(act, s_halo, t)
                    nc.scalar.activation(xp[:, m, HALO:], b[:], ACT.Copy).then_inc(s_ad, 1)

                def dt_copy(w):
                    b = item(w, "dt")
                    nc.scalar.activation(dtT[0:HEADS, :], b[0:HEADS, :], ACT.Copy).then_inc(s_ad, 1)

                def softplus(step, t):
                    act.wait_ge(s_dtv, t + 1)
                    step.link(nc.scalar.activation(ab_dt, v_dt, ACT.Abs))
                    step.link(nc.scalar.activation(e_dt, ab_dt, ACT.Exp, scale=-1.0))
                    nc.scalar.activation(ln_dt, e_dt, ACT.Ln, bias=eps[:, 2:3]).then_inc(s_dtl, 1)

                def z_silu(w, t, c):
                    b = item(w, f"z{c}")
                    if c == 0:
                        ge(act, s_y, CH * t)
                    nc.scalar.activation(z_s[:, c, :], b[:], ACT.Silu).then_inc(s_ad, 1)

                def conv_silu(t, n):
                    m = CONV_ORDER[n]
                    act.wait_ge(s_cv, MC * t + n + 1)
                    nc.scalar.activation(xc[:, m, :], xc[:, m, :], ACT.Silu,
                                         bias=conv_b_sb[:, m:m + 1]).then_inc(s_xc, 1)

                def pre(w, i, c):
                    b = item(w, f"xt{c}")
                    if c >= 2:
                        act.wait_ge(s_u, 3 * (CH * i + c - 1))
                    nc.scalar.activation(xt[:, c % 2, :], b[:], ACT.Copy).then_inc(s_ad, 1)
                    for half, name in enumerate(("dlo", "dhi")):
                        b = item(w, f"{name}{c}")
                        if c >= 2:
                            act.wait_ge(s_di, w.dve(f"ydiag{c - 2}") + 1)
                        dst = E[:, c % 2, half * 4:half * 4 + 4, :].rearrange("p h l -> p (h l)")
                        nc.scalar.activation(dst, b[:], ACT.Exp).then_inc(s_ad, 1)

                def gate_rms(step, w, i, c):
                    act.wait_ge(s_y, CH * i + c + 1)
                    step.link(nc.scalar.activation(junk[:], y[:, c % 2, :], ACT.Square,
                                                   accum_out=ssy[:, c:c + 1]))
                    step.link(nc.scalar.activation(lny[:, c:c + 1], ssy[:, c:c + 1], ACT.Ln,
                                                   scale=1.0 / INNER, bias=eps[:, 1:2]))
                    nc.scalar.activation(rsy[:, c:c + 1], lny[:, c:c + 1], ACT.Exp, scale=-0.5).then_inc(s_rsy, 1)

                def yT(w, c):
                    hi_part(w, f"yT{c}", flat3(yT_hi))

                def low_sum(i, n):
                    act.wait_ge(s_low, CHECKS * i + n + 1)
                    nc.scalar.activation(low[:].bitcast(F32), low[:], ACT.Copy,
                                         accum_out=lowsum[:, bass.ds(CHECKS * i + n, 1)]).then_inc(s_sum, 1)

                def hT(w):
                    for k in range(KD):
                        hi_part(w, f"hT{k}", hT_hi[:, k, :])

                def h_rms(step, w):
                    act.wait_ge(s_dd, w.dve(f"wo{CH - 1}") + 1 + DVE_BANKS)
                    for c in range(CH):
                        step.link(nc.scalar.activation(junk[:, 0:D], h[:, c, :], ACT.Square,
                                                       accum_out=ssh[:, c:c + 1]))
                    step.link(nc.scalar.activation(lnh, ssh, ACT.Ln, scale=1.0 / D, bias=eps[:, 0:1]))
                    nc.scalar.activation(r2h, lnh, ACT.Exp, scale=-1.0).then_inc(s_r2h, 1)

                def fc(w, i, j):
                    b = item(w, f"fc{j}")
                    if j >= 2:
                        m_split(act, i, j - 2)
                    m = m_fc[:, j % 2, :]
                    nc.scalar.activation(m, b[:], ACT.Relu).then_inc(s_ad, 1)
                    act.wait_ge(s_ad, w.act(f"fc{j}") + 1 + ACT_BANKS)
                    nc.scalar.activation(m, m, ACT.Square).then_inc(s_m, 1)
                    if j >= 2:
                        act.wait_ge(s_pj, KH * i + j - 1)
                    act.wait_ge(s_m, KH * i + j + 1)
                    nc.scalar.activation(m_hi[:, j % 2, :], m, ACT.Copy).then_inc(s_mh, 1)

                def iteration(w, i, more):
                    per = C_STEPS + X_STEPS + DT_STEPS
                    step = Steps(act, s_as, X_STEPS + DT_STEPS + per * i)
                    act.preload_act_table_set(LOG_EXP)
                    b = item(w, "cums")
                    nc.scalar.activation(dec[:].rearrange("p n c -> p (n c)"), b[:, 0:3 * CH * HEADS],
                                         ACT.Exp).then_inc(s_ad, 1)
                    pre(w, i, 0)
                    for c in range(CH):
                        if c < CH - 1:
                            pre(w, i, c + 1)
                        if c > 0:
                            yT(w, c - 1)
                            gate_rms(step, w, i, c - 1)
                        low_sum(i, c)
                        if more and c == 1:
                            x_rms(step, i + 1)
                        if more and c == TURN_XN:
                            xnT(w)
                    if more:
                        dt_copy(w)
                        xbc(w, i + 1, 4)
                    yT(w, CH - 1)
                    gate_rms(step, w, i, CH - 1)
                    if more:
                        xbc(w, i + 1, 5)
                        xbc(w, i + 1, 0)
                        xbc(w, i + 1, 1)
                        softplus(step, i + 1)
                    hT(w)
                    if more:
                        xbc(w, i + 1, 2)
                        xbc(w, i + 1, 3)
                    h_rms(step, w)
                    for j in range(KH):
                        fc(w, i, j)
                        if more and j < CH:
                            z_silu(w, i + 1, j)
                        if more and j < 2:
                            conv_silu(i + 1, j)
                        if more and 2 <= j < MC:
                            conv_silu(i + 1, j)
                    assert step.n == (per if more else C_STEPS), step.n

                step = Steps(act, s_as, 0)
                act.preload_act_table_set(LOG_EXP)
                act.wait_ge(s_masks, MASKS)
                x_rms(step, 0)
                act.wait_ge(s_stage[0], 16)
                nc.scalar.activation(flat3(w_in_hi), staged[0][0], ACT.Copy).then_inc(s_whi, 1)
                w = Where(FIRST, 0)
                xnT(w)
                act.wait_ge(s_params, 96)
                nc.scalar.activation(neg_a[:], a_log_b[:], ACT.Exp).then_inc(s_nega, 1)
                act.wait_ge(s_wlo, 1)
                dt_copy(w)
                for m in CONV_ORDER:
                    xbc(w, 0, m)
                softplus(step, 0)
                for n in range(1, len(staged)):
                    act.wait_ge(s_stage[n], 16)
                    if n == 1:
                        act.wait_ge(s_nw, KI)
                    nc.scalar.activation(flat3(staged[n][1]), staged[n][0], ACT.Copy).then_inc(s_whi, 1)
                for c in range(CH):
                    z_silu(w, 0, c)
                for n in range(MC):
                    conv_silu(0, n)
                act.wait_ge(s_wlo, len(staged))
                assert step.n == X_STEPS + DT_STEPS
                with act.Fori(0, TILES - 1) as i:
                    iteration(Where(LOOP, i), i, True)
                iteration(Where(LAST, TILES - 1), TILES - 1, False)

            @block.gpsimd
            def _(pool):
                pool.memset(ident[:], 0.0).then_inc(s_masks, 1)
                pool.memset(ones[:], 1.0).then_inc(s_masks, 1)
                for n, v in enumerate((EPS_OUT, EPS_GATE, 1.0, -0.5)):
                    pool.memset(eps[:, n:n + 1], v).then_inc(s_masks, 1)
                pool.memset(S[:, 0, :], 0.0).then_inc(s_masks, 1)
                pool.memset(dtT[:], 0.0).then_inc(s_masks, 1)
                pool.wait_ge(s_masks, 2)
                pool.affine_select(out=ident[:], in_=ident[:], compare_op=ALU.not_equal, fill=1.0, base=0,
                                   pattern=[[-1, P]], channel_multiplier=1).then_inc(s_masks, 1)
                pool.affine_select(out=tri_le[:], in_=ones[:], compare_op=ALU.is_ge, fill=0.0, base=0,
                                   pattern=[[1, P]], channel_multiplier=-1).then_inc(s_masks, 1)
                pool.affine_select(out=tri_gt[:], in_=ones[:], compare_op=ALU.is_gt, fill=0.0, base=0,
                                   pattern=[[-1, P]], channel_multiplier=1).then_inc(s_masks, 1)
                pool.memset(rsv[:], 0.0).then_inc(s_masks, 1)
                for n in range(1, len(staged)):
                    st, hi, lo, _ = staged[n]
                    pool.wait_ge(s_wlo, n)
                    pool.wait_ge(s_whi, n + 1)
                    nc.gpsimd.tensor_tensor(flat3(lo), st, flat3(hi).bitcast(F32), ALU.subtract).then_inc(s_wlo, 1)
                bc = lambda ap: ap.unsqueeze(2).broadcast_to([P, HEADS, HDIM])
                heads = lambda ap: ap.rearrange("p (h d) -> p h d", h=HEADS)

                def masked_a(w, i, c):
                    if c >= 2:
                        pool.wait_ge(s_ai, w.act(f"dhi{c - 2}") + 1)
                    nc.gpsimd.tensor_tensor(
                        RA[:, c % 2, :, :],
                        a[:, c * HEADS:(c + 1) * HEADS].unsqueeze(2).broadcast_to([P, HEADS, P]),
                        tri_le[:].unsqueeze(1).broadcast_to([P, HEADS, P]), ALU.mult).then_inc(s_ra, 1)

                def iteration(w, i, more):
                    for c in range(CH):
                        b, o = c % 2, 1 - c % 2
                        if c < CH - 1:
                            masked_a(w, i, c + 1)
                        hs = slice(c * HEADS, (c + 1) * HEADS)
                        pool.wait_ge(s_ad, w.act(f"xt{c}") + 1 + ACT_BANKS)
                        if c >= 2:
                            pool.wait_ge(s_si, CH * i + c - 1)
                        nc.gpsimd.tensor_tensor(heads(u[:, b, :]), heads(xt[:, b, :]), bc(dt[:, hs]),
                                                ALU.mult).then_inc(s_u, 1)
                        pool.wait_ge(s_u, 3 * (CH * i + c) + 1)
                        nc.gpsimd.tensor_tensor(heads(ud[:, b, :]), heads(u[:, b, :]), bc(dec[:, 1, hs]),
                                                ALU.mult).then_inc(s_u, 1)
                        if c >= 2:
                            pool.wait_ge(s_rsy, CH * i + c - 1)
                            pool.wait_ge(s_di, w.dve(f"yT{c - 2}") + 1)
                        nc.gpsimd.tensor_tensor(heads(y[:, b, :]), heads(xt[:, b, :]), bc(dskip_b[:]),
                                                ALU.mult).then_inc(s_u, 1)
                        pool.wait_ge(s_sup, CH * i + c + 1)
                        nc.gpsimd.tensor_tensor(heads(S[:, o, :]), heads(S[:, b, :]), bc(dec[:, 2, hs]),
                                                ALU.mult).then_inc(s_sdec, 1)
                    for j in range(CH):
                        pool.wait_ge(s_mh, KH * i + j + 1)
                        nc.gpsimd.tensor_tensor(m_lo[:, j % 2, :], m_fc[:, j % 2, :], m_hi[:, j % 2, :].bitcast(F32),
                                                ALU.subtract).then_inc(s_ml, 1)
                    if more:
                        pool.wait_ge(s_a, i + 2)
                        masked_a(w, i + 1, 0)
                    pool.wait_ge(s_mv, i + 1)
                    nc.gpsimd.tensor_tensor(rsv[:], mv[:, 1, :], eps[:, 3:4].broadcast_to([P, CH]),
                                            ALU.pow).then_inc(s_rsv, 1)

                pool.wait_ge(s_a, 1)
                masked_a(Where(FIRST, 0), 0, 0)
                with pool.Fori(0, TILES - 1) as i:
                    iteration(Where(LOOP, i), i, True)
                iteration(Where(LAST, TILES - 1), TILES - 1, False)

            @block.vector
            def _(dve):
                dve.sem_inc(s_dd, DVE_BANKS)
                dve.sem_inc(s_sup, 1)
                dve.sem_inc(s_pjd, 1)
                heads = lambda ap: ap.rearrange("p (h d) -> p h d", h=HEADS)
                per_chunk = lambda ap: ap.unsqueeze(1).broadcast_to([P, CH, HEADS])
                chunks = lambda ap: ap.rearrange("p (c h) -> p c h", c=CH)
                F_STEPS = MC * (TAPS - 1) + 4
                CM_STEPS = 2 * CH + 2 + STAT_STEPS

                def item(w, name):
                    dve.wait_ge(s_di, w.dve(name) + 1)
                    return banks[w.dve_bank(name)]

                def lo_part(w, name, hi, lo):
                    dve.wait_ge(s_hi, w.hi(name) + 1)
                    nc.vector.tensor_tensor(lo, banks[w.dve_bank(name)][:], hi.bitcast(F32),
                                            ALU.subtract).then_inc(s_dd, 1)

                def norm_x(t):
                    dve.wait_ge(s_rsx, t + 1)
                    for c in range(CH):
                        nc.vector.tensor_scalar(xn[:, c, :], x_in[:, c, :], rsx[:, c:c + 1], None,
                                                ALU.mult).then_inc(s_xn, 1)

                def xnT(w):
                    for k in range(KD):
                        lo_part(w, f"xnT{k}", xnT_hi[:, k, :], xnT_lo[:, k, :])

                def taps(step, w, t, ms):
                    marks = {}
                    for tap in range(TAPS):
                        for m in ms:
                            src = xp[:, m, tap:tap + TILE]
                            cw = conv_w_sb[:, m, tap:tap + 1]
                            if tap == 0:
                                dve.wait_ge(s_ad, w.act(f"xbc{m}") + 1 + ACT_BANKS)
                                marks[m] = step.mark(nc.vector.tensor_scalar(xc[:, m, :], src, cw, None, ALU.mult))
                                continue
                            step.wait(marks[m])
                            ins = nc.vector.scalar_tensor_tensor(out=xc[:, m, :], in0=src, scalar=cw,
                                                                 in1=xc[:, m, :], op0=ALU.mult, op1=ALU.add)
                            if tap == TAPS - 1:
                                ins.then_inc(s_cv, 1)
                            else:
                                marks[m] = step.mark(ins)

                def bias_dt(t):
                    dve.wait_ge(s_dtt, t + 1)
                    nc.vector.tensor_tensor(chunks(v_dt), st_bank[:].rearrange("p (c n) -> p c n", c=CH)[:, :, 0:HEADS], per_chunk(dt_bias_b[:]),
                                            ALU.add).then_inc(s_dtv, 1)

                def dt_and_a(step, t):
                    dve.wait_ge(s_dtl, t + 1)
                    step.link(nc.vector.tensor_scalar(c_dt, e_dt, 1.0, -1.0, ALU.add, ALU.add))
                    step.link(nc.vector.tensor_tensor(r_dt, e_dt, c_dt, ALU.subtract))
                    step.link(nc.vector.tensor_tensor(l_dt, ln_dt, r_dt, ALU.add))
                    step.link(nc.vector.scalar_tensor_tensor(out=dt, in0=v_dt, scalar=0.0, in1=l_dt,
                                                             op0=ALU.max, op1=ALU.add))
                    nc.vector.tensor_tensor(chunks(a), chunks(dt), per_chunk(neg_a[:]), ALU.mult).then_inc(s_a, 1)

                def halo(t):
                    dve.wait_ge(s_cv, MC * t + MC)
                    k = keep[:, bass.ds(t, 1)].unsqueeze(2).broadcast_to([P, MC, HALO])
                    nc.vector.tensor_tensor(xp[:, :, 0:HALO].bitcast(I32), xp[:, :, TILE:].bitcast(I32), k,
                                            ALU.bitwise_and).then_inc(s_halo, 1)

                def pre(step, w, i, c):
                    b = item(w, f"gb{c}")
                    if c >= 2:
                        dve.wait_ge(s_si, CH * i + c - 1)
                    g = step.mark(nc.vector.tensor_tensor(Gm[:, c % 2, :], b[:, 0:P], tri_le[:], ALU.mult))
                    nc.vector.tensor_copy(Bt[:, c % 2, :], b[:, P:2 * P]).then_inc(s_dd, 1)
                    dve.wait_ge(s_ad, w.act(f"dhi{c}") + 1 + ACT_BANKS)
                    step.wait(g)
                    e = E[:, c % 2, :, :]
                    nc.vector.tensor_tensor(e, e, Gm[:, c % 2, :].unsqueeze(1).broadcast_to([P, HEADS, P]),
                                            ALU.mult).then_inc(s_M, 1)

                def main(step, w, i, c):
                    yc, hs = y[:, c % 2, :], slice(c * HEADS, (c + 1) * HEADS)
                    b = item(w, f"yoff{c}")
                    dve.wait_ge(s_u, 3 * (CH * i + c) + 3)
                    nc.vector.tensor_tensor(heads(tmp[:]), heads(b[:]),
                                            dec[:, 0, hs].unsqueeze(2).broadcast_to([P, HEADS, HDIM]),
                                            ALU.mult).then_inc(s_dd, 1)
                    b = item(w, f"ydiag{c}")
                    step.link(nc.vector.tensor_tensor(yc, yc, b[:], ALU.add))
                    nc.vector.tensor_tensor(tmp[:], tmp[:], yc, ALU.add).then_inc(s_dd, 1)
                    dve.wait_ge(s_si, CH * i + c + 1)
                    dve.wait_ge(s_sdec, CH * i + c + 1)
                    o = S[:, 1 - c % 2, :]
                    ins = nc.vector.tensor_tensor(o, o, st_bank[:], ALU.add)
                    if c < CH - 1:
                        ins.then_inc(s_sup, 1)
                    else:
                        step.link(ins)
                        nc.vector.tensor_tensor(o.bitcast(I32), o.bitcast(I32),
                                                keep[:, bass.ds(i, 1)].broadcast_to([P, INNER]),
                                                ALU.bitwise_and).then_inc(s_sup, 1)
                    dve.wait_ge(s_dd, w.dve(f"ydiag{c}") + 1 + DVE_BANKS)
                    nc.vector.tensor_tensor(yc, tmp[:], z_s[:, c, :], ALU.mult).then_inc(s_y, 1)

                def yT(w, c):
                    lo_part(w, f"yT{c}", flat3(yT_hi), flat3(yT_lo))

                def add_out(w, i, c):
                    b = item(w, f"wo{c}")
                    dve.wait_ge(s_rsy, CH * i + c + 1)
                    dve.wait_ge(s_xres, i + 1)
                    nc.vector.scalar_tensor_tensor(out=h[:, c, :], in0=b[:, 0:D], scalar=rsy[:, c:c + 1],
                                                   in1=x_res[:, c, :], op0=ALU.mult, op1=ALU.add).then_inc(s_dd, 1)

                def low_bits(i, n):
                    if n == 0:
                        dve.wait_ge(s_chk, 16 * i + 16)
                    if n > 0:
                        dve.wait_ge(s_sum, CHECKS * i + n)
                    nc.vector.tensor_scalar(low[:], chk[:, n * LOW:(n + 1) * LOW].bitcast(I32), LOW_BITS, None,
                                            ALU.bitwise_and).then_inc(s_low, 1)

                def hT(w):
                    for k in range(KD):
                        lo_part(w, f"hT{k}", hT_hi[:, k, :], hT_lo[:, k, :])

                def m_lo_part(i, j):
                    dve.wait_ge(s_mh, KH * i + j + 1)
                    nc.vector.tensor_tensor(m_lo[:, j % 2, :], m_fc[:, j % 2, :], m_hi[:, j % 2, :].bitcast(F32),
                                            ALU.subtract).then_inc(s_mld, 1)

                def x_plus_h(step, w):
                    dve.wait_ge(s_dd, w.dve("hT1") + 1 + DVE_BANKS)
                    step.mark(nc.vector.tensor_tensor(x_res[:], x_res[:], h[:], ALU.add))
                    return step.n

                def norm_x1(step, i, xh):
                    dve.wait_ge(s_pj, KH * i + KH)
                    dve.wait_ge(s_r2h, i + 1)
                    dve.wait_ge(s_x1o, 16 * i + 1)
                    step.wait(xh)
                    for c in range(CH):
                        nc.vector.scalar_tensor_tensor(
                            out=x1[:, c, :], in0=pj_banks[c // 2][:, (c % 2) * D:(c % 2 + 1) * D],
                            scalar=r2h[:, c:c + 1], in1=x_res[:, c, :], op0=ALU.mult, op1=ALU.add).then_inc(s_pjd, 1)
                    dve.wait_ge(s_pjd, CH * i + CH + 1)
                    layer_norm_stats(step, x1, bn, mv, EPS_LN).then_inc(s_mv, 1)

                def scale_x1(i):
                    dve.wait_ge(s_rsv, i + 1)
                    for c in range(CH):
                        nc.vector.tensor_scalar(x1[:, c, :], x1[:, c, :], mv[:, 0, c:c + 1], rsv[:, c:c + 1],
                                                ALU.subtract, ALU.mult).then_inc(s_x1, 1)

                def keep_x(t):
                    nc.vector.tensor_copy(x_res[:], x_in[:]).then_inc(s_xres, 1)

                def iteration(w, i, more):
                    per = F_STEPS + CM_STEPS
                    step = Steps(dve, s_ds, F_STEPS + per * i)
                    pre(step, w, i, 0)
                    for c in range(CH):
                        low_bits(i, c)
                        if c < CH - 1:
                            pre(step, w, i, c + 1)
                        if c > 0:
                            yT(w, c - 1)
                        if more and c == TURN_XN:
                            norm_x(i + 1)
                        main(step, w, i, c)
                        if c > 0:
                            add_out(w, i, c - 1)
                        if more and c == TURN_XN:
                            xnT(w)
                    yT(w, CH - 1)
                    if more:
                        bias_dt(i + 1)
                        taps(step, w, i + 1, (4,))
                    add_out(w, i, CH - 1)
                    hT(w)
                    xh = x_plus_h(step, w)
                    if more:
                        taps(step, w, i + 1, (5,))
                        taps(step, w, i + 1, (0, 1))
                        dt_and_a(step, i + 1)
                        taps(step, w, i + 1, (2, 3))
                        halo(i + 1)
                    for j in range(CH, KH):
                        m_lo_part(i, j)
                    norm_x1(step, i, xh)
                    if more:
                        keep_x(i + 1)
                    scale_x1(i)
                    assert step.n == (per if more else CM_STEPS), step.n

                dve.wait_ge(s_stage[1], 16)
                dve.wait_ge(s_params, 96)
                for k in range(KI):
                    part = staged[1][0][:, k * D:(k + 1) * D]
                    nc.vector.tensor_scalar(part, part, norm_w_sb[:, k:k + 1], None, ALU.mult).then_inc(s_nw, 1)
                nc.vector.memset(keep[:], -1).then_inc(s_start, 1)
                for n, t in enumerate(range(SEQ_TILES - 1, TILES, SEQ_TILES)):
                    dve.wait_ge(s_start, n + 1)
                    nc.vector.memset(keep[:, t:t + 1], 0).then_inc(s_start, 1)
                step = Steps(dve, s_ds, 0)
                norm_x(0)
                dve.wait_ge(s_x, 16)
                keep_x(0)
                w = Where(FIRST, 0)
                dve.wait_ge(s_whi, 1)
                nc.vector.tensor_tensor(flat3(w_in_lo), staged[0][0], flat3(w_in_hi).bitcast(F32),
                                        ALU.subtract).then_inc(s_wlo, 1)
                xnT(w)
                dve.wait_ge(s_wlo, 1)
                nc.vector.memset(xp[:, :, 0:HALO], 0.0).then_inc(s_start, 1)
                dve.wait_ge(s_nega, 1)
                nc.vector.tensor_scalar(neg_a[:], neg_a[:], -1.0, None, ALU.mult).then_inc(s_nega, 1)
                dve.wait_ge(s_start, 2 + TILES // SEQ_TILES)
                bias_dt(0)
                taps(step, w, 0, (4, 5))
                taps(step, w, 0, (0, 1))
                dve.wait_ge(s_nega, 2)
                dt_and_a(step, 0)
                taps(step, w, 0, (2, 3))
                halo(0)
                assert step.n == F_STEPS
                with dve.Fori(0, TILES - 1) as i:
                    iteration(Where(LOOP, i), i, True)
                iteration(Where(LAST, TILES - 1), TILES - 1, False)

        a_ctx.close()

        w1_sb, w2_sb = sb("w1_sb", [P, KD, HID], F32R), sb("w2_sb", [P, KD, HID], F32R)
        h1_sb, h2_sb = sb("h1_sb", [P, KH, HID], F32R), sb("h2_sb", [P, KH, HID], F32R)
        w3_sb = sb("w3_sb", [P, KH, D], F32R)
        scale = sb("scale", [P, 4, KH])
        s3_b = sb("s3_b", [P, D])
        x1_in, x1_res = sb("x1_in", [P, CH, D]), sb("x1_res", [P, CH, D])
        x1T_hi, x1T_lo = sb("x1T_hi", [P, KD, TILE], F32R), sb("x1T_lo", [P, KD, TILE], F32R)
        hA_hi, hA_lo = sb("hA_hi", [P, KH, TILE], F32R), sb("hA_lo", [P, KH, TILE], F32R)
        hB_hi, hB_lo = sb("hB_hi", [P, KH, TILE], F32R), sb("hB_lo", [P, KH, TILE], F32R)
        FULL = 3
        TURN, BEHIND = KH - 2, 3
        full = sb("full", [P, FULL, TILE])
        gate = sb("gate", [P, 2, TILE])
        o_sb = sb("o_sb", [P, CH, D])
        low_all = sb("low_all", [P, 1])
        inexact = sb("inexact", [1, 2])
        bn_b, mv_b = sb("bn_b", [P, CH, 6]), sb("mv_b", [P, 3, CH])
        rsv_b = sb("rsv_b", [P, CH])

        t_bank = lambda i: banks[B_ACT_BANKS + i % B_DVE_BANKS]
        g_bank = lambda i: banks[i % B_ACT_BANKS]
        acc = banks[6:8]

        s_par = sem("ffn_params_loaded")
        s_h1 = sem("h1_loaded")
        s_h2 = sem("h2_loaded")
        s_w3 = sem("w3_loaded")
        s_w = [sem(f"{n}_loaded") for n in ("w1", "w2")]
        s_all = sem("low_bits_added")
        s_flagp = sem("inexact_summed")
        s_flag = sem("inexact_ready")
        s_x1i = sem("x1_loaded")
        s_kept = sem("x1_kept")
        s_ti = sem("ffn_dve_item_ready")
        s_td = sem("ffn_dve_item_drained")
        s_gi = sem("ffn_act_item_ready")
        s_gd = sem("ffn_act_item_drained")
        s_thi = sem("x1T_hi_ready")
        s_shi = sem("hidden_hi_ready")
        s_ghi = sem("gated_hi_ready")
        s_split = sem("hidden_split")
        s_acc = sem("ffn_sum_ready")
        s_accd = sem("ffn_sum_drained")
        s_bstep = sem("ffn_dve_step")
        s_mvb = sem("out_var_ready")
        s_rsb = sem("out_rstd_ready")
        s_o = sem("out_ready")
        s_store = sem("out_stored")

        with nc.Block() as block:
            @block.sync
            def _(sp):
                def load(at):
                    sp.dma_start(x1_in[:], rows(x1_dram, at)).then_inc(s_x1i, 16)

                def store(i, at):
                    sp.wait_ge(s_o, CH * i + CH)
                    sp.dma_start(rows(out, at), o_sb[:]).then_inc(s_store, 16)

                def weights(name, dst, s):
                    at, k, n = FFN_COLS[name]
                    sp.dma_start(flat3(dst).bitcast(F32), raw[:, at:at + k * n]).then_inc(s, 16)

                sp.sem_inc(s_store, 1)
                load(0)
                weights("w1", w1_sb, s_w[0])
                weights("w2", w2_sb, s_w[1])
                for n, s in enumerate((s1, s2, sh1, sh2)):
                    sp.dma_start(scale[:, n, :], s).then_inc(s_par, 16)
                sp.dma_start(s3_b[:], s3.partition_broadcast(P)).then_inc(s_par, 16)
                weights("h1", h1_sb, s_h1)
                weights("h2", h2_sb, s_h2)
                weights("w3", w3_sb, s_w3)
                sp.wait_ge(s_kept, 1)
                sp.wait_ge(s_td, KD + B_DVE_BANKS)
                load(TILE * D)
                with sp.Fori(0, TILES - 2) as i:
                    at, at_next = sp.snap(i * (TILE * D)), sp.snap((i + 2) * (TILE * D))
                    store(i, at)
                    sp.wait_ge(s_kept, i + 2)
                    load(at_next)
                store(TILES - 2, (TILES - 2) * TILE * D)
                store(TILES - 1, (TILES - 1) * TILE * D)
                sp.wait_ge(s_store, 16 * TILES + 1)

            @block.tensor
            def _(pe):
                def act_item(i, n):
                    pe.wait_ge(s_gd, NBA * i + n + 1)
                    return g_bank(n)

                def dve_item(i, n):
                    pe.wait_ge(s_td, NBD * i + KD + n + 1)
                    return t_bank(KD + n)

                def turn(t):
                    pe.wait_ge(s_x1i, 16 * t + 16)
                    for k in range(KD):
                        b = dve_item(t, k - KD)
                        for c in range(CH):
                            last = pe.transpose(b[:, c * P:(c + 1) * P], x1_in[:, c, k * P:(k + 1) * P], ident[:])
                        last.then_inc(s_ti, 1)

                def tile(i, exact, more, first):
                    def two(o, w, hi, lo, first, last, rows_out=False):
                        for n, v in enumerate((lo, hi)):
                            ww, vv = (w, v) if exact else (w.bitcast(F32), v.bitcast(F32))
                            a_, b_ = (vv, ww) if rows_out else (ww, vv)
                            ins = pe.matmul(o, a_, b_, start=first and n == 0, stop=last and n == 1,
                                            skip_group_check=True)
                        return ins

                    pe.wait_ge(s_td, NBD * i + KD + B_DVE_BANKS)
                    for j in range(KH):
                        cols = slice(j * P, (j + 1) * P)
                        for w, b, s in ((w1_sb, act_item(i, j), s_gi), (w2_sb, dve_item(i, j), s_ti)):
                            for k in range(KD):
                                last = two(b[:], w[:, k, cols], x1T_hi[:, k, :], x1T_lo[:, k, :], k == 0, k == KD - 1)
                            last.then_inc(s, 1)

                    def channel(layer, w, hi, lo, j):
                        b = act_item(i, layer * KH + j)
                        cols = slice(j * P, (j + 1) * P)
                        for k in range(KH):
                            if j == 0:
                                pe.wait_ge(s_split, 3 * KH * i + (layer - 1) * KH + k + 1)
                            last = two(b[:], w[:, k, cols], hi[:, k, :], lo[:, k, :], k == 0, k == KH - 1)
                        last.then_inc(s_gi, 1)

                    def out_rows(j):
                        pe.wait_ge(s_split, 3 * KH * i + 2 * KH + j + 1)
                        if j == 0:
                            pe.wait_ge(s_accd, 2 * i + 1)
                        for c in range(CH):
                            tok = slice(c * P, (c + 1) * P)
                            last = two(acc[c // 2][:, (c % 2) * D:(c % 2 + 1) * D], w3_sb[:, j, :], hA_hi[:, j, tok],
                                       hA_lo[:, j, tok], j == 0 and c % 2 == 0, j == KH - 1, rows_out=True)
                        last.then_inc(s_acc, 1)

                    if first:
                        pe.wait_ge(s_h1, 16)
                    for j in range(KH):
                        channel(1, h1_sb, hA_hi, hA_lo, j)
                    if first:
                        pe.wait_ge(s_h2, 16)
                        pe.wait_ge(s_w3, 16)
                    for j in range(KH):
                        if more and j == TURN:
                            turn(i + 1)
                        channel(2, h2_sb, hB_hi, hB_lo, j)
                        if j >= BEHIND:
                            out_rows(j - BEHIND)
                    for j in range(KH - BEHIND, KH):
                        out_rows(j)

                pe.wait_ge(s_w[0], 16)
                pe.wait_ge(s_w[1], 16)
                turn(0)
                pe.wait_ge(s_all, 1)
                pe.matmul(banks[0][0:1, 0:2], low_all[:], ones[:, 0:2], start=True, stop=True).then_inc(s_flagp, 1)
                pe.wait_ge(s_flag, 1)
                bits = pe.value_load(inexact[0:1, 0:1].bitcast(I32))

                def tiles(exact):
                    tile(0, exact, True, True)
                    with pe.Fori(1, TILES - 1) as i:
                        tile(i, exact, True, False)
                    tile(TILES - 1, exact, False, False)

                with pe.If(bits == 0):
                    tiles(True)
                with pe.Else():
                    tiles(False)

            @block.scalar
            def _(act):
                act.sem_inc(s_gd, B_ACT_BANKS)
                act.wait_ge(s_par, 80)

                def turned(t):
                    for k in range(KD):
                        act.wait_ge(s_ti, NBD * t + k + 1)
                        nc.scalar.activation(x1T_hi[:, k, :], t_bank(k)[:], ACT.Copy).then_inc(s_thi, 1)

                def tile(i, more):
                    def item(n):
                        act.wait_ge(s_gi, NBA * i + n + 1)
                        return g_bank(n)

                    def gate_hi(j):
                        act.wait_ge(s_td, NBD * i + KD + j + 1 + B_DVE_BANKS)
                        nc.scalar.activation(hA_hi[:, j, :], full[:, j % FULL, :], ACT.Copy).then_inc(s_ghi, 1)

                    for j in range(KH):
                        b = item(j)
                        nc.scalar.activation(gate[:, j % 2, :], b[:], ACT.Silu, scale=scale[:, 0, j:j + 1]).then_inc(s_gd, 1)
                        if j > 0:
                            gate_hi(j - 1)
                    gate_hi(KH - 1)
                    for n in range(KH, 3 * KH):
                        b = item(n)
                        act.wait_ge(s_split, 3 * KH * i + n - FULL + 1)
                        nc.scalar.activation(full[:, n % FULL, :], b[:], ACT.Gelu,
                                             scale=scale[:, 1 + n // KH, n % KH:n % KH + 1]).then_inc(s_gd, 1)
                        if more and n == 2 * KH + TURN - 1:
                            turned(i + 1)

                turned(0)
                with act.Fori(0, TILES - 1) as i:
                    tile(i, True)
                tile(TILES - 1, False)

            @block.gpsimd
            def _(pool):
                with pool.Fori(0, TILES) as i:
                    pool.wait_ge(s_mvb, i + 1)
                    nc.gpsimd.tensor_tensor(rsv_b[:], mv_b[:, 1, :], eps[:, 3:4].broadcast_to([P, CH]),
                                            ALU.pow).then_inc(s_rsb, 1)

            @block.vector
            def _(dve):
                dve.sem_inc(s_td, B_DVE_BANKS)
                dve.sem_inc(s_accd, 1)
                nc.vector.reduce_sum(low_all[:], lowsum[:], AX.X).then_inc(s_all, 1)
                dve.wait_ge(s_flagp, 1)
                nc.vector.tensor_copy(inexact[:], banks[0][0:1, 0:2]).then_inc(s_flag, 1)
                dve.wait_ge(s_par, 80)
                B_STEPS = 2 + STAT_STEPS

                def turned(t):
                    for k in range(KD):
                        dve.wait_ge(s_thi, KD * t + k + 1)
                        nc.vector.tensor_tensor(x1T_lo[:, k, :], t_bank(k)[:], x1T_hi[:, k, :].bitcast(F32),
                                                ALU.subtract).then_inc(s_td, 1)

                def keep_rows(t):
                    nc.vector.tensor_copy(x1_res[:], x1_in[:]).then_inc(s_kept, 1)

                def tile(i, more, first):
                    def lo(n, hi, lo):
                        nc.vector.tensor_tensor(lo, full[:, n % FULL, :], hi.bitcast(F32), ALU.subtract).then_inc(s_split, 1)

                    def gated(j):
                        dve.wait_ge(s_ti, NBD * i + KD + j + 1)
                        dve.wait_ge(s_gd, NBA * i + j + 1 + B_ACT_BANKS)
                        if j >= FULL:
                            dve.wait_ge(s_split, 3 * KH * i + j - FULL + 1)
                        nc.vector.scalar_tensor_tensor(out=full[:, j % FULL, :], in0=t_bank(KD + j)[:],
                                                       scalar=scale[:, 1, j:j + 1], in1=gate[:, j % 2, :],
                                                       op0=ALU.mult, op1=ALU.mult).then_inc(s_td, 1)

                    def gated_lo(j):
                        dve.wait_ge(s_ghi, KH * i + j + 1)
                        lo(j, hA_hi[:, j, :], hA_lo[:, j, :])

                    for j in range(KH):
                        gated(j)
                        if j > 0:
                            gated_lo(j - 1)
                    gated_lo(KH - 1)
                    if not first:
                        finish(i - 1, True)
                    for n in range(KH, 3 * KH):
                        dve.wait_ge(s_gd, NBA * i + n + 1 + B_ACT_BANKS)
                        hi, lo_ = (hB_hi, hB_lo) if n < 2 * KH else (hA_hi, hA_lo)
                        nc.vector.tensor_copy(hi[:, n % KH, :], full[:, n % FULL, :]).then_inc(s_shi, 1)
                        dve.wait_ge(s_shi, 2 * KH * i + n - KH + 1)
                        lo(n, hi[:, n % KH, :], lo_[:, n % KH, :])
                        if more and n == 2 * KH + TURN - 1:
                            turned(i + 1)

                def finish(i, more):
                    step = Steps(dve, s_bstep, B_STEPS * i)
                    dve.wait_ge(s_acc, KH * i + KH)
                    dve.wait_ge(s_store, 16 * i + 1)
                    for n in range(2):
                        nc.vector.tensor_tensor(o_sb[:, 2 * n:2 * n + 2, :], acc[n][:].rearrange("p (c n) -> p c n", c=2),
                                                s3_b[:].unsqueeze(1).broadcast_to([P, 2, D]), ALU.mult).then_inc(s_accd, 1)
                    for n in range(2):
                        o = o_sb[:, 2 * n:2 * n + 2, :]
                        dve.wait_ge(s_accd, 2 * i + n + 2)
                        step.mark(nc.vector.tensor_tensor(o, o, x1_res[:, 2 * n:2 * n + 2, :], ALU.add))
                    step.wait(step.n)
                    layer_norm_stats(step, o_sb, bn_b, mv_b, EPS_LN).then_inc(s_mvb, 1)
                    assert step.n == B_STEPS
                    if more:
                        keep_rows(i + 1)
                    dve.wait_ge(s_rsb, i + 1)
                    for c in range(CH):
                        nc.vector.tensor_scalar(o_sb[:, c, :], o_sb[:, c, :], mv_b[:, 0, c:c + 1], rsv_b[:, c:c + 1],
                                                ALU.subtract, ALU.mult).then_inc(s_o, 1)

                dve.wait_ge(s_x1i, 16)
                keep_rows(0)
                turned(0)
                tile(0, True, True)
                with dve.Fori(1, TILES - 1) as i:
                    tile(i, True, False)
                tile(TILES - 1, False, False)
                finish(TILES - 1, False)


def kernel(**inputs):
    import numpy as np
    import concourse.bacc as bacc
    from concourse.bass_utils import run_bass_kernel_spmd as run

    get = lambda name: np.asarray(inputs[name])
    channels = lambda v: np.ascontiguousarray(v.reshape(-1, P).T)
    matrix = lambda v: v.T.reshape(-1, P, v.shape[0]).transpose(1, 0, 2).reshape(P, -1)
    x = get("L0_attn_x")
    batch, seq, width = x.shape
    f, g = "L0_attn_", "L0_ffn_"
    arrays = {
        "x": x.reshape(-1, width),
        "w_in": get(f + "w_in"),
        "conv_w": np.ascontiguousarray(get(f + "conv_w").reshape(-1, P, TAPS).transpose(1, 0, 2)),
        "conv_b": channels(get(f + "conv_b")),
        "dt_bias": get(f + "dt_bias"),
        "a_log": get(f + "a_log"),
        "d_skip": get(f + "d_skip"),
        "norm_w": channels(get(f + "norm_w")),
        "w_out": get(f + "w_out"),
        "w_fc": get(f + "w_fc"),
        "w_proj": get(f + "w_proj"),
        "w_ffn": np.concatenate([matrix(get(g + n + "_w")) for n in FFN_COLS], axis=1),
        "s1": channels(get(g + "w1_s")),
        "s2": channels(get(g + "w2_s")),
        "sh1": channels(get(g + "h1_s")),
        "sh2": channels(get(g + "h2_s")),
        "s3": get(g + "w3_s"),
    }
    arrays = {n: np.ascontiguousarray(a) for n, a in arrays.items()}
    nc = bacc.Bacc("TRN2", target_bir_lowering=False, num_devices=1)
    args = [nc.dram_tensor(n, a.shape, mybir.dt.from_np(a.dtype), kind="ExternalInput").ap()
            for n, a in arrays.items()]
    out = nc.dram_tensor("out", arrays["x"].shape, F32, kind="ExternalOutput").ap()
    post_ln_block(nc, *args, out, seq)
    r = run(nc, [arrays], core_ids=[0])
    return r.results[0]["out"].reshape(batch, seq, width)
```
